# Optimizing a Trainium2 kernel written in Bass

```python
import numpy as np
import jax
import jax.numpy as jnp

def _softmax(x, axis=-1):
    return jax.nn.softmax(x, axis=axis)

def _gelu(x):
    return jax.nn.gelu(x, approximate=True)

def _silu(x):
    return jax.nn.silu(x)

def _sigmoid(x):
    return jax.nn.sigmoid(x)

def _layernorm(x, axis=-1, eps=1e-05):
    m = jnp.mean(x, axis=axis, keepdims=True)
    v = jnp.var(x, axis=axis, keepdims=True)
    return (x - m) / jnp.sqrt(v + eps)

def _scatter_add(tgt, idx, src, axis=0):
    return tgt.at[idx].add(src)

def _segment_sum(src, seg, n):
    return jax.ops.segment_sum(src, seg, n)
kernel_name = 'mk_metaformer_d1_conv_nchw256_r4_3e5cf8'

def setup_inputs(seed: int=0):
    np.random.seed(seed)
    _w = jnp.asarray

    def _rec_inputs():
        import jax
        import jax.numpy as jnp
        _gk = jax.random.key(seed)
        x = -0.0002928 + 1 * jax.random.normal(jax.random.fold_in(_gk, 1), (4, 64, 16, 16), jnp.float32)
        return x
    x = _rec_inputs()

    def _L0_conv_setup():
        import jax, jax.numpy as jnp
        import numpy as np
        B, C, H, W = (4, 64, 16, 16)
        D = 16
        key = jax.random.key(seed)
        ks = jax.random.split(key, 7)
        s_in = 1.0 / np.sqrt(C)
        return {'x': jax.random.normal(ks[0], (B, C, H, W), dtype=jnp.float32), 'wq': jax.random.uniform(ks[1], (D, C), jnp.float32, -s_in, s_in), 'bq': jax.random.uniform(ks[2], (D,), jnp.float32, -s_in, s_in), 'wk': jax.random.uniform(ks[3], (D, C), jnp.float32, -s_in, s_in), 'bk': jax.random.uniform(ks[4], (D,), jnp.float32, -s_in, s_in), 'wv': jax.random.uniform(ks[5], (C, C), jnp.float32, -s_in, s_in), 'bv': jax.random.uniform(ks[6], (C,), jnp.float32, -s_in, s_in)}
    _L0_conv_all = _L0_conv_setup()
    _L0_conv_in = {k: v for k, v in _L0_conv_all.items() if k in ('wq', 'bq', 'wk', 'bk', 'wv', 'bv')}
    del _L0_conv_all

    def _L0_ffn_setup():
        import jax, jax.numpy as jnp
        import numpy as np
        TOP_K = 2
        LN_EPS = 1e-05
        key = jax.random.key(seed)
        ks = jax.random.split(key, 8)
        B, S, D, E, H = (16, 256, 64, 8, 256)
        x = jax.random.normal(ks[0], (B, S, D), dtype=jnp.float32)
        Wr = jax.random.normal(ks[1], (D, E), dtype=jnp.float32) * 0.1
        br = jnp.zeros((E,), dtype=jnp.float32)
        ln_g = jnp.ones((E, D), dtype=jnp.float32)
        ln_b = jnp.zeros((E, D), dtype=jnp.float32)
        W1 = jax.random.normal(ks[2], (E, D, H), dtype=jnp.float32) * (1.0 / np.sqrt(D))
        b1 = jnp.zeros((E, H), dtype=jnp.float32)
        W2 = jax.random.normal(ks[3], (E, H, D), dtype=jnp.float32) * (1.0 / np.sqrt(H))
        b2 = jnp.zeros((E, D), dtype=jnp.float32)
        return {'x': x, 'Wr': Wr, 'br': br, 'ln_g': ln_g, 'ln_b': ln_b, 'W1': W1, 'b1': b1, 'W2': W2, 'b2': b2}
    _L0_ffn_all = _L0_ffn_setup()
    _L0_ffn_in = {k: v for k, v in _L0_ffn_all.items() if k in ('Wr', 'br', 'ln_g', 'ln_b', 'W1', 'b1', 'W2', 'b2')}
    del _L0_ffn_all
    return {'x': x, 'L0_conv_wq': _L0_conv_in['wq'], 'L0_conv_bq': _L0_conv_in['bq'], 'L0_conv_wk': _L0_conv_in['wk'], 'L0_conv_bk': _L0_conv_in['bk'], 'L0_conv_wv': _L0_conv_in['wv'], 'L0_conv_bv': _L0_conv_in['bv'], 'L0_ffn_Wr': _L0_ffn_in['Wr'], 'L0_ffn_br': _L0_ffn_in['br'], 'L0_ffn_ln_g': _L0_ffn_in['ln_g'], 'L0_ffn_ln_b': _L0_ffn_in['ln_b'], 'L0_ffn_W1': _L0_ffn_in['W1'], 'L0_ffn_b1': _L0_ffn_in['b1'], 'L0_ffn_W2': _L0_ffn_in['W2'], 'L0_ffn_b2': _L0_ffn_in['b2']}

def reference(x, L0_conv_wq, L0_conv_bq, L0_conv_wk, L0_conv_bk, L0_conv_wv, L0_conv_bv, L0_ffn_Wr, L0_ffn_br, L0_ffn_ln_g, L0_ffn_ln_b, L0_ffn_W1, L0_ffn_b1, L0_ffn_W2, L0_ffn_b2):
    import jax
    import jax.numpy as jnp

    def _L0_conv_ref(x, wq, bq, wk, bk, wv, bv):
        import jax, jax.numpy as jnp
        import numpy as np
        B, C, H, W = (4, 64, 16, 16)
        D = 16
        b, c, h, w = x.shape
        xf = x.reshape(b, c, h * w)
        q = jnp.einsum('dc,bcn->bnd', wq, xf) + bq
        k = jnp.einsum('dc,bcn->bdn', wk, xf) + bk[:, None]
        v = jnp.einsum('oc,bcn->bon', wv, xf) + bv[:, None]
        attn = jax.nn.softmax(jnp.einsum('bnd,bdm->bnm', q, k), axis=-1)
        out = jnp.einsum('bcm,bnm->bcn', v, attn)
        return out.reshape(b, c, h, w)

    def _L0_ffn_ref(x, Wr, br, ln_g, ln_b, W1, b1, W2, b2):
        import jax, jax.numpy as jnp
        import numpy as np
        TOP_K = 2
        LN_EPS = 1e-05
        B, S, D = x.shape
        N = B * S
        xt = x.reshape(N, D)
        logits = xt @ Wr + br
        probs = jax.nn.softmax(logits, axis=-1)
        top_p, top_idx = jax.lax.top_k(probs, TOP_K)
        weights = top_p / top_p.sum(axis=-1, keepdims=True)
        mu = xt.mean(axis=-1, keepdims=True)
        var = ((xt - mu) ** 2).mean(axis=-1, keepdims=True)
        xn = (xt - mu) * jax.lax.rsqrt(var + LN_EPS)
        xe = xn[None, :, :] * ln_g[:, None, :] + ln_b[:, None, :]
        h = jax.nn.gelu(jnp.einsum('end,edh->enh', xe, W1) + b1[:, None, :], approximate=False)
        y = jnp.einsum('enh,ehd->end', h, W2) + b2[:, None, :]
        y_tok = jnp.transpose(y, (1, 0, 2))
        sel = jnp.take_along_axis(y_tok, top_idx[:, :, None], axis=1)
        out = (weights[:, :, None] * sel).sum(axis=1)
        return out.reshape(B, S, D)

    def _gn(v, G=32, eps=1e-05):
        B_, C_, H_, W_ = v.shape
        g = v.reshape(B_, G, C_ // G, H_, W_)
        m = jnp.mean(g, axis=(2, 3, 4), keepdims=True)
        s = jnp.var(g, axis=(2, 3, 4), keepdims=True)
        return ((g - m) / jnp.sqrt(s + eps)).reshape(v.shape)

    def _ln_c(v, eps=1e-06):
        m = jnp.mean(v, axis=1, keepdims=True)
        s = jnp.var(v, axis=1, keepdims=True)
        return (v - m) / jnp.sqrt(s + eps)

    def _ln_t(v, eps=1e-05):
        m = jnp.mean(v, axis=-1, keepdims=True)
        s = jnp.var(v, axis=-1, keepdims=True)
        return (v - m) / jnp.sqrt(s + eps)

    def _to_tokens(v):
        B_, C_, H_, W_ = v.shape
        return v.reshape(B_, C_, H_ * W_).transpose(0, 2, 1)

    def _from_tokens(t, like):
        B_, C_, H_, W_ = like.shape
        return t.transpose(0, 2, 1).reshape(B_, C_, H_, W_)
    x = x + _L0_conv_ref(_ln_c(x), L0_conv_wq, L0_conv_bq, L0_conv_wk, L0_conv_bk, L0_conv_wv, L0_conv_bv)
    t = _to_tokens(x)
    t = t + _L0_ffn_ref(_ln_t(t), L0_ffn_Wr, L0_ffn_br, L0_ffn_ln_g, L0_ffn_ln_b, L0_ffn_W1, L0_ffn_b1, L0_ffn_W2, L0_ffn_b2)
    x = _from_tokens(t, x)
    return x

_drawn_inputs = setup_inputs


def setup_inputs(seed=0):
    import zlib

    import numpy as np

    out = dict(_drawn_inputs(seed))
    spreads = {'L0_ffn_br': (0.0, 0.1),
     'L0_ffn_ln_g': (1.0, 0.2),
     'L0_ffn_ln_b': (0.0, 0.1),
     'L0_ffn_b1': (0.0, 0.1),
     'L0_ffn_b2': (0.0, 0.1)}
    factors = {}
    for name, (base, spread) in spreads.items():
        noise = np.random.default_rng([zlib.crc32(name.encode()), seed]).standard_normal(out[name].shape)
        drawn = base * np.exp(spread * noise) if base else spread * noise
        out[name] = jnp.asarray(drawn.astype(out[name].dtype))
    for name, factor in factors.items():
        out[name] = (out[name] * factor).astype(out[name].dtype)
    return out
```

```python
from contextlib import ExitStack

import concourse.bass as bass
from concourse import mybir

F32 = mybir.dt.float32
F16 = mybir.dt.float16
U32 = mybir.dt.uint32
ALU = mybir.AluOpType
ACT = mybir.ActivationFunctionType
AX_X = mybir.AxisListType.X

P = 128
IMAGES, C, PIX = 4, 64, 256
D = 16
E, HID = 8, 256
HALVES = 2
IMG = IMAGES // HALVES
TOK = IMG * PIX
TILES = TOK // P
PT = PIX // P
J = HID // P
UNITS = E * J
CA = C + 1
EPS_C, EPS_T = 1e-6, 1e-5
SX = 2.0 ** 8
SW = 2.0 ** 8
SG = 2.0 ** -8
RING = 4
FFN_LOADS = 9
LAG = 3


def cast_on_act(g):
    return g % 4 != 3


def sub_on_pool(g):
    return g % 2 == 1


def count(which, g):
    return sum(1 for i in range(g + 1) if which(i))


def build_block(nc, x, wq, bq, wk, bk, wv, bv, wr, br, ln_g, ln_b, w1, b1, w2, b2, out):
    with ExitStack() as ctx:
        def sb(name, shape, dt=F32):
            return ctx.enter_context(nc.sbuf_tensor(name, shape, dt))

        def sem(name):
            return ctx.enter_context(nc.semaphore(name))

        banks = ctx.enter_context(nc.psum_tensor("banks", [P, 8, 512], F32))
        BK = [[banks[:, 4 * h + i, :] for i in range(4)] for h in range(HALVES)]
        ps_xT = [BK[h][0][:, 0:TILES * C].rearrange("p (t c) -> p t c", t=TILES) for h in range(HALVES)]
        ps_xn = [BK[h][1] for h in range(HALVES)]
        ps_G = [BK[h][2] for h in range(HALVES)]
        ps_V = [BK[h][3][:, 0:TILES * C].rearrange("p (t c) -> p t c", t=TILES) for h in range(HALVES)]
        ps_S = [[BK[h][i].rearrange("p (t m) -> p t m", t=PT) for i in range(IMG)] for h in range(HALVES)]
        ps_PT = [[BK[h][2 + i] for i in range(IMG)] for h in range(HALVES)]
        ps_O = [BK[h][0].rearrange("p (t c) -> p t c", t=TILES) for h in range(HALVES)]
        ps_F = [BK[h][1] for h in range(HALVES)]
        ps_L = [BK[h][2][:, 0:TILES * E].rearrange("p (t e) -> p t e", t=TILES) for h in range(HALVES)]
        ps_wT = [BK[h][3] for h in range(HALVES)]
        ps_B2 = [BK[h][2][:, 0:TILES * C].rearrange("p (t c) -> p t c", t=TILES) for h in range(HALVES)]
        ps_z = [BK[0][0], BK[0][1]]
        ps_y = [BK[0][2 + i].rearrange("p (t c) -> p t c", t=TILES) for i in range(2)]
        ps_out = [BK[1][h] for h in range(HALVES)]
        ps_AT = BK[0][2][0:CA, 0:CA]
        ps_WvT = BK[0][3][0:CA, 0:C]
        ps_gb = BK[1][3][:, 0:2 * E]
        ps_b1 = BK[1][3][:, 0:2 * UNITS].rearrange("p (k j e) -> p k j e", k=2, j=J)

        X = sb("X", [C, IMAGES, PIX])
        WqA = sb("WqA", [D, CA])
        WkA = sb("WkA", [D, CA])
        WvA = sb("WvA", [C, CA])
        WrF = sb("WrF", [P, E])
        WrS = sb("WrS", [P, E], F16)
        brB = sb("brB", [P, E])
        GB = sb("GB", [2 * E, P])
        gT = sb("gT", [P, 2 * E])
        b1R = sb("b1R", [E, HID])
        b1C = sb("b1C", [P, 2, J, E])
        b1S = sb("b1S", [P, J, E])
        b2F = sb("b2F", [E, C])
        b2S = sb("b2S", [E, C])
        W1F = sb("W1F", [P, E, HID])
        W1G = sb("W1G", [P, E, HID])
        W1S = sb("W1S", [P, E, J, P], F16)
        W2F = sb("W2F", [P, E, J, C])
        W2S = sb("W2S", [P, E, J, 2, C], F16)
        ident = sb("ident", [P, P])
        iota = sb("iota", [P, E])
        half = sb("half", [P, 2 * TILES])
        AT = sb("AT", [CA, CA])
        WvT = sb("WvT", [CA, C])

        def both(name, shape, dt=F32):
            return [sb(f"{name}{h}", shape, dt) for h in range(HALVES)]

        xT = both("xT", [P, TILES, C])
        st = both("st", [P, TILES, 6])
        mv = both("mv", [P, TILES, 2])
        base1 = both("base1", [P, TILES])
        rs1 = both("rs1", [P, TILES])
        XnT = both("XnT", [P, TILES, CA])
        XN = both("XN", [CA, TOK])
        GS = both("GS", [CA, TOK])
        VT = both("VT", [P, TILES, CA])
        nmax = both("nmax", [P, TILES])
        PR = both("PR", [P, TILES, PIX])
        PTs = both("PTs", [P, IMG, PT, PIX])
        rsum = both("rsum", [P, TILES])
        T = both("T", [P, TILES, C])
        st2 = both("st2", [P, TILES, 6])
        mv2 = both("mv2", [P, TILES, 2])
        base2 = both("base2", [P, 2, TILES])
        rs2 = both("rs2", [P, 2, TILES])
        rs2s = both("rs2s", [P, TILES])
        X2 = both("X2", [P, TILES, 2, C])
        XH = both("XH", [P, TOK], F16)
        XL = both("XL", [P, TOK], F16)
        inv2 = both("inv2", [P, TILES])
        ratio = both("ratio", [P, TILES])
        LG = both("LG", [P, TILES, E])
        top = both("top", [P, TILES, 8])
        topi = both("topi", [P, TILES, 8], U32)
        topf = both("topf", [P, TILES, 2])
        gap = both("gap", [P, TILES])
        th = both("th", [P, TILES])
        wab = both("wab", [P, 2, TILES])
        hot = both("hot", [P, 2, TILES, E])
        gate = both("gate", [P, TILES, E])
        part = both("part", [P, 2, TILES, E])
        gateT = both("gateT", [E, TOK])
        acc = both("acc", [P, TILES, 2, C])
        fin = both("fin", [P, TILES, C])
        OUT = both("OUT", [C, TOK])
        H32 = sb("H32", [P, RING, TOK])
        HH = sb("HH", [P, RING, TOK], F16)
        HL = sb("HL", [P, RING, TOK], F16)

        x_in = [sem(f"x_in{h}") for h in range(HALVES)]
        qkv_in = sem("qkv_in")
        ffn_in = sem("ffn_in")
        w1_in = [sem(f"w1_in{e}") for e in range(E // 2)]
        w2_in = sem("w2_in")
        out_done = [sem(f"out_done{h}") for h in range(HALVES)]
        pool_step = sem("pool_step")
        consts_ready = sem("consts_ready")
        vec_step = sem("vec_step")
        AT_ps = sem("AT_ps")
        WvT_ps = sem("WvT_ps")
        AT_ready = sem("AT_ready")
        WvT_ready = sem("WvT_ready")
        gT_ps = sem("gT_ps")
        gT_ready = sem("gT_ready")
        b1_ps = sem("b1_ps")
        b1_ready = sem("b1_ready")
        b2_ready = sem("b2_ready")
        Wr_ready = sem("Wr_ready")
        W1_scaled = sem("W1_scaled")
        W1_hi = sem("W1_hi")
        W1_ready = sem("W1_ready")
        W2_hi = sem("W2_hi")
        W2_ready = sem("W2_ready")
        xT_ps = sem("xT_ps")
        var1_ready = sem("var1_ready")
        rs1_ready = sem("rs1_ready")
        xnT_ready = sem("xnT_ready")
        xT_copied = sem("xT_copied")
        xn_ps = sem("xn_ps")
        xn_ready = sem("xn_ready")
        G_ps = sem("G_ps")
        G_ready = sem("G_ready")
        V_ps = sem("V_ps")
        V_ready = sem("V_ready")
        S_ps = sem("S_ps")
        nmax_ready = sem("nmax_ready")
        prob_ready = sem("prob_ready")
        PT_ps = sem("PT_ps")
        PT_act = sem("PT_act")
        PT_dve = sem("PT_dve")
        O_ps = sem("O_ps")
        var2_ready = sem("var2_ready")
        rs2_ready = sem("rs2_ready")
        rs2b_ready = sem("rs2b_ready")
        x2_ready = sem("x2_ready")
        F_ps = sem("F_ps")
        XH_ready = sem("XH_ready")
        XL_ready = sem("XL_ready")
        L_ps = sem("L_ps")
        gap_ready = sem("gap_ready")
        th_ready = sem("th_ready")
        gate_ready = sem("gate_ready")
        wT_ps = sem("wT_ps")
        gateT_ready = sem("gateT_ready")
        B2_ps = sem("B2_ps")
        acc_ready = sem("acc_ready")
        z_ready = sem("z_ready")
        h32_ready = sem("h32_ready")
        hh_act = sem("hh_act")
        hh_dve = sem("hh_dve")
        hl_pool = sem("hl_pool")
        hl_dve = sem("hl_dve")
        layer2_done = sem("layer2_done")
        y_used = sem("y_used")
        fin_ready = sem("fin_ready")
        out_ps = sem("out_ps")
        out_ready = sem("out_ready")

        block = ctx.enter_context(nc.Block())

        def wait_hh(eng, g):
            if cast_on_act(g):
                eng.wait_ge(hh_act, count(cast_on_act, g))
            else:
                eng.wait_ge(hh_dve, g + 1 - count(cast_on_act, g))

        def wait_hl(eng, g):
            if sub_on_pool(g):
                eng.wait_ge(hl_pool, count(sub_on_pool, g))
            else:
                eng.wait_ge(hl_dve, g + 1 - count(sub_on_pool, g))

        @block.sync
        def _(sp):
            for h in range(HALVES):
                sp.dma_start(X[:, IMG * h:IMG * (h + 1), :],
                             x[IMG * h:IMG * (h + 1)].rearrange("b c y z -> c b (y z)")).then_inc(x_in[h], 16)
            sp.dma_start(WqA[:, 0:C], wq).then_inc(qkv_in, 16)
            sp.dma_start(WqA[:, C:CA], bq.rearrange("(d a) -> d a", a=1)).then_inc(qkv_in, 16)
            sp.dma_start(WkA[:, 0:C], wk).then_inc(qkv_in, 16)
            sp.dma_start(WkA[:, C:CA], bk.rearrange("(d a) -> d a", a=1)).then_inc(qkv_in, 16)
            sp.dma_start(WvA[:, 0:C], wv).then_inc(qkv_in, 16)
            sp.dma_start(WvA[:, C:CA], bv.rearrange("(d a) -> d a", a=1)).then_inc(qkv_in, 16)
            for k in range(2):
                sp.dma_start(GB[0:E, C * k:C * k + C], ln_g).then_inc(ffn_in, 16)
                sp.dma_start(GB[E:2 * E, C * k:C * k + C], ln_b).then_inc(ffn_in, 16)
                sp.dma_start(WrF[C * k:C * k + C, :], wr).then_inc(ffn_in, 16)
            sp.dma_start(b1R[:, :], b1).then_inc(ffn_in, 16)
            sp.dma_start(b2F[:, :], b2).then_inc(ffn_in, 16)
            sp.dma_start(brB[:, :], br.rearrange("(a e) -> a e", a=1).broadcast_to([P, E])).then_inc(ffn_in, 16)
            for q in range(E // 2):
                for k in range(2):
                    sp.dma_start(W1F[C * k:C * k + C, 2 * q:2 * q + 2, :],
                                 w1[2 * q:2 * q + 2].rearrange("e d h -> d e h")).then_inc(w1_in[q], 16)
                if q == 0:
                    sp.dma_start(W2F[:, :, :, :].rearrange("p e j d -> p e (j d)"),
                                 w2.rearrange("e (p j) d -> p e (j d)", j=J)).then_inc(w2_in, 16)
            for h in range(HALVES):
                sp.wait_ge(out_ready, h + 1)
                sp.dma_start(out[IMG * h:IMG * (h + 1)].rearrange("b c y z -> c b (y z)"),
                             OUT[h][:, :].rearrange("c (b n) -> c b n", b=IMG)).then_inc(out_done[h], 16)
            for h in range(HALVES):
                sp.wait_ge(out_done[h], 16)

        @block.gpsimd
        def _(pool):
            nc.gpsimd.memset(ident[:, :], 0.0).then_inc(pool_step, 1)
            pool.wait_ge(pool_step, 1)
            nc.gpsimd.affine_select(out=ident[:, :], in_=ident[:, :], compare_op=ALU.not_equal, fill=1.0,
                                    base=0, pattern=[[-1, P]], channel_multiplier=1)\
                .then_inc(consts_ready, 1)
            nc.gpsimd.memset(half[:, :], -0.5).then_inc(consts_ready, 1)
            for h in range(HALVES):
                last = nc.gpsimd.memset(XnT[h][:, :, C:CA], 1.0)
            last.then_inc(consts_ready, 1)
            for h in range(HALVES):
                nc.gpsimd.memset(VT[h][:, :, C:CA], 1.0)
                nc.gpsimd.memset(acc[h][:, :, 1, :], 0.0)
            for e in range(E):
                last = nc.gpsimd.memset(iota[:, e:e + 1], float(e))
            last.then_inc(consts_ready, 1)
            for h in range(HALVES):
                pool.wait_ge(var1_ready, h + 1)
                if h == 0:
                    pool.wait_ge(consts_ready, 2)
                nc.gpsimd.tensor_tensor(rs1[h][:, :], base1[h][:, :], half[:, 0:TILES], ALU.pow)\
                    .then_inc(rs1_ready, 1)

            def scale_w1(q):
                pool.wait_ge(w1_in[q], 32)
                if q == 0:
                    pool.wait_ge(gT_ready, 1)
                es = slice(2 * q, 2 * q + 2)
                nc.gpsimd.tensor_tensor(W1G[:, es, :], W1F[:, es, :],
                                        gT[:, es].unsqueeze(2).broadcast_to([P, 2, HID]),
                                        ALU.mult).then_inc(W1_scaled, 1)

            scale_w1(0)
            scale_w1(1)
            for h in range(HALVES):
                pool.wait_ge(var2_ready, h + 1)
                nc.gpsimd.tensor_tensor(rs2[h][:, 0, :], base2[h][:, 0, :], half[:, 0:TILES], ALU.pow)\
                    .then_inc(rs2_ready, 1)
                nc.gpsimd.tensor_tensor(rs2[h][:, 1, :], base2[h][:, 1, :], half[:, 0:TILES], ALU.pow)\
                    .then_inc(rs2b_ready, 1)
            scale_w1(2)
            scale_w1(3)

            for g in range(HALVES * UNITS):
                if sub_on_pool(g):
                    r = g % RING
                    pool.wait_ge(h32_ready, g + 1)
                    wait_hh(pool, g)
                    if g >= RING:
                        pool.wait_ge(layer2_done, g - RING + 1)
                    nc.gpsimd.tensor_tensor(HL[:, r, :], H32[:, r, :], HH[:, r, :], ALU.subtract)\
                        .then_inc(hl_pool, 1)

        @block.scalar
        def _(act):
            act.wait_ge(AT_ps, 1)
            nc.scalar.copy(AT[:, :], ps_AT).then_inc(AT_ready, 1)
            act.wait_ge(WvT_ps, 1)
            nc.scalar.copy(WvT[:, :], ps_WvT).then_inc(WvT_ready, 1)
            for h in range(HALVES):
                act.wait_ge(xn_ps, h + 1)
                nc.scalar.copy(XN[h][:, :], ps_xn[h][0:CA, :]).then_inc(xn_ready, 1)
                act.wait_ge(xnT_ready, h + 1)
                nc.scalar.copy(xT[h][:, :, :], ps_xT[h]).then_inc(xT_copied, 1)
            for h in range(HALVES):
                act.wait_ge(G_ps, h + 1)
                nc.scalar.copy(GS[h][:, :], ps_G[h][0:CA, :]).then_inc(G_ready, 1)
            for h in range(HALVES):
                for i in range(IMG):
                    act.wait_ge(nmax_ready, IMG * h + i + 1)
                    for t in range(PT):
                        k = PT * i + t
                        last = nc.scalar.activation(PR[h][:, k, :], ps_S[h][i][:, t, :], ACT.Exp,
                                                    bias=nmax[h][:, k:k + 1])
                    last.then_inc(prob_ready, 1)
            for h in range(HALVES):
                act.wait_ge(PT_ps, IMG * h + 1)
                nc.scalar.copy(PTs[h][:, 0, :, :], ps_PT[h][0].rearrange("p (t n) -> p t n", t=PT))\
                    .then_inc(PT_act, 1)

            def split_w1(q):
                act.wait_ge(W1_scaled, q + 1)
                for e in range(2 * q, 2 * q + 2):
                    last = nc.scalar.copy(W1S[:, e, :, :], W1G[:, e, :].rearrange("p (m j) -> p j m", j=J))
                last.then_inc(W1_hi, 1)

            split_w1(0)
            act.wait_ge(w2_in, 16)
            nc.scalar.mul(W2S[:, :, :, 0, :], W2F[:, :, :, :], SW).then_inc(W2_hi, 1)
            split_w1(1)
            for h in range(HALVES):
                act.wait_ge(F_ps, h + 1)
                nc.scalar.copy(XH[h][:, :], ps_F[h]).then_inc(XH_ready, 1)
            for h in range(HALVES):
                act.wait_ge(gap_ready, h + 1)
                nc.scalar.activation(th[h][:, :], gap[h][:, :], ACT.Tanh, scale=0.5).then_inc(th_ready, 1)
                act.wait_ge(wT_ps, h + 1)
                nc.scalar.copy(gateT[h][:, :], ps_wT[h][0:E, :]).then_inc(gateT_ready, 1)
            split_w1(2)
            split_w1(3)

            def output(h):
                act.wait_ge(out_ps, h + 1)
                nc.scalar.copy(OUT[h][:, :], ps_out[h][0:C, :]).then_inc(out_ready, 1)

            act.wait_ge(b1_ready, 1)
            for g in range(HALVES * UNITS):
                e, j = (g % UNITS) // J, g % J
                r = g % RING
                if g == UNITS + 8:
                    output(0)
                act.wait_ge(z_ready, g + 1)
                if g >= RING:
                    wait_hl(act, g - RING)
                    act.wait_ge(layer2_done, g - RING + 1)
                if cast_on_act(g):
                    nc.scalar.activation(HH[:, r, :], ps_z[g % 2], ACT.Gelu, bias=b1S[:, j, e:e + 1],
                                         scale=1.0 / (SX * SW)).then_inc(hh_act, 1)
                nc.scalar.activation(H32[:, r, :], ps_z[g % 2], ACT.Gelu, bias=b1S[:, j, e:e + 1],
                                     scale=1.0 / (SX * SW)).then_inc(h32_ready, 1)
            output(1)

        @block.vector
        def _(dve):
            chain = [0]

            def step(ins):
                chain[0] += 1
                ins.then_inc(vec_step, 1)
                dve.wait_ge(vec_step, chain[0])

            def stats(src, s6, m2):
                for t in range(TILES):
                    last = nc.vector.bn_stats(s6[:, t, :], src[:, t, :])
                step(last)
                for t in range(TILES):
                    last = nc.vector.bn_aggr(m2[:, t, :], s6[:, t, :])
                step(last)

            for h in range(HALVES):
                dve.wait_ge(xT_ps, h + 1)
                stats(ps_xT[h], st[h], mv[h])
                nc.vector.tensor_scalar(base1[h][:, :], mv[h][:, :, 1], EPS_C, None, ALU.add)\
                    .then_inc(var1_ready, 1)
            dve.wait_ge(gT_ps, 1)
            nc.vector.tensor_scalar(gT[:, 0:E], ps_gb[:, 0:E], SW, None, ALU.mult)
            nc.vector.tensor_copy(gT[:, E:2 * E], ps_gb[:, E:2 * E]).then_inc(gT_ready, 1)
            for h in range(HALVES):
                dve.wait_ge(rs1_ready, h + 1)
                if h == 0:
                    dve.wait_ge(consts_ready, 3)
                for t in range(TILES):
                    last = nc.vector.tensor_scalar(XnT[h][:, t, 0:C], ps_xT[h][:, t, :], mv[h][:, t, 0:1],
                                                   rs1[h][:, t:t + 1], ALU.subtract, ALU.mult)
                last.then_inc(xnT_ready, 1)
            dve.wait_ge(ffn_in, 16 * FFN_LOADS)
            step(nc.vector.tensor_scalar(WrS[:, :], WrF[:, :], SW, None, ALU.mult))
            nc.vector.scalar_tensor_tensor(out=WrS[C:P, :], in0=WrF[C:P, :], scalar=SW, in1=WrS[C:P, :],
                                           op0=ALU.mult, op1=ALU.subtract).then_inc(Wr_ready, 1)
            nc.vector.tensor_scalar(b2S[:, :], b2F[:, :], 1.0 / SG, None, ALU.mult).then_inc(b2_ready, 1)
            for h in range(HALVES):
                dve.wait_ge(V_ps, h + 1)
                if h == 0:
                    dve.wait_ge(consts_ready, 4)
                nc.vector.tensor_copy(VT[h][:, :, 0:C], ps_V[h]).then_inc(V_ready, 1)
            for h in range(HALVES):
                for i in range(IMG):
                    dve.wait_ge(S_ps, IMG * h + i + 1)
                    nc.vector.tensor_reduce(nmax[h][:, PT * i:PT * i + PT], ps_S[h][i], AX_X, ALU.max,
                                            negate=True).then_inc(nmax_ready, 1)
            for h in range(HALVES):
                dve.wait_ge(PT_ps, IMG * h + 2)
                nc.vector.tensor_copy(PTs[h][:, 1, :, :], ps_PT[h][1].rearrange("p (t n) -> p t n", t=PT))\
                    .then_inc(PT_dve, 1)

            def rest_w1(q):
                dve.wait_ge(W1_hi, q + 1)
                for e in range(2 * q, 2 * q + 2):
                    last = nc.vector.tensor_tensor(W1S[C:P, e, :, :],
                                                   W1G[C:P, e, :].rearrange("p (m j) -> p j m", j=J),
                                                   W1S[C:P, e, :, :], ALU.subtract)
                last.then_inc(W1_ready, 1)

            for h in range(HALVES):
                dve.wait_ge(O_ps, h + 1)
                step(nc.vector.reciprocal(rsum[h][:, :], ps_O[h][:, :, C]))
                dve.wait_ge(xT_copied, h + 1)
                for t in range(TILES):
                    last = nc.vector.scalar_tensor_tensor(out=T[h][:, t, :], in0=ps_O[h][:, t, 0:C],
                                                          scalar=rsum[h][:, t:t + 1], in1=xT[h][:, t, :],
                                                          op0=ALU.mult, op1=ALU.add)
                step(last)
                stats(T[h], st2[h], mv2[h])
                nc.vector.tensor_scalar(base2[h][:, 0, :], mv2[h][:, :, 1], 1.0 + EPS_T, EPS_T * EPS_T,
                                        ALU.mult, ALU.add)
                nc.vector.tensor_scalar(base2[h][:, 1, :], mv2[h][:, :, 1], EPS_T, None, ALU.add)\
                    .then_inc(var2_ready, 1)
            rest_w1(0)
            for h in range(HALVES):
                dve.wait_ge(rs2_ready, h + 1)
                step(nc.vector.tensor_scalar(rs2s[h][:, :], rs2[h][:, 0, :], SX, None, ALU.mult))
                for t in range(TILES):
                    last = nc.vector.tensor_scalar(X2[h][:, t, :, :],
                                                   T[h][:, t, :].unsqueeze(1).broadcast_to([P, 2, C]),
                                                   mv2[h][:, t, 0:1],
                                                   rs2s[h][:, t:t + 1], ALU.subtract, ALU.mult)
                last.then_inc(x2_ready, 1)
            dve.wait_ge(W2_hi, 1)
            nc.vector.scalar_tensor_tensor(out=W2S[:, :, :, 1, :].rearrange("p e j d -> p (e j) d"),
                                           in0=W2F[:, :, :, :].rearrange("p e j d -> p (e j) d"), scalar=SW,
                                           in1=W2S[:, :, :, 0, :].rearrange("p e j d -> p (e j) d"),
                                           op0=ALU.mult, op1=ALU.subtract).then_inc(W2_ready, 1)
            for h in range(HALVES):
                dve.wait_ge(XH_ready, h + 1)
                nc.vector.tensor_tensor(XL[h][:, :], ps_F[h], XH[h][:, :], ALU.subtract).then_inc(XL_ready, 1)
            rest_w1(1)
            dve.wait_ge(b1_ps, 1)
            step(nc.vector.tensor_copy(b1C[:, :, :, :], ps_b1))
            nc.vector.tensor_tensor(b1S[:, :, :], b1C[:, 0, :, :], b1C[:, 1, :, :], ALU.add).then_inc(b1_ready, 1)
            for h in range(HALVES):
                dve.wait_ge(rs2b_ready, h + 1)
                step(nc.vector.reciprocal(inv2[h][:, :], rs2s[h][:, :]))
                step(nc.vector.scalar_tensor_tensor(out=ratio[h][:, :], in0=rs2[h][:, 1, :], scalar=1.0 / SW,
                                                    in1=inv2[h][:, :], op0=ALU.mult, op1=ALU.mult))
                dve.wait_ge(L_ps, h + 1)
                for t in range(TILES):
                    last = nc.vector.scalar_tensor_tensor(out=LG[h][:, t, :], in0=ps_L[h][:, t, :],
                                                          scalar=ratio[h][:, t:t + 1], in1=brB[:, :],
                                                          op0=ALU.mult, op1=ALU.add)
                step(last)
                for t in range(TILES):
                    last = nc.vector.max(top[h][:, t, :], LG[h][:, t, :])
                step(last)
                nc.vector.tensor_tensor(gap[h][:, :], top[h][:, :, 0], top[h][:, :, 1], ALU.subtract)\
                    .then_inc(gap_ready, 1)
                for t in range(TILES):
                    last = nc.vector.max_index(topi[h][:, t, :], top[h][:, t, :], LG[h][:, t, :])
                step(last)
                step(nc.vector.tensor_copy(topf[h][:, :, :], topi[h][:, :, 0:2]))
                for k in range(2):
                    last = nc.vector.tensor_tensor(hot[h][:, k, :, :],
                                                   iota[:, :].unsqueeze(1).broadcast_to([P, TILES, E]),
                                                   topf[h][:, :, k:k + 1].broadcast_to([P, TILES, E]),
                                                   ALU.is_equal)
                dve.wait_ge(th_ready, h + 1)
                for k in range(2):
                    last = nc.vector.tensor_scalar(wab[h][:, k, :], th[h][:, :], (0.5 - k) * SG, 0.5 * SG,
                                                   ALU.mult, ALU.add)
                step(last)
                for k in range(2):
                    last = nc.vector.tensor_tensor(part[h][:, k, :, :], hot[h][:, k, :, :],
                                                   wab[h][:, k, :].unsqueeze(2).broadcast_to([P, TILES, E]),
                                                   ALU.mult)
                step(last)
                nc.vector.tensor_tensor(gate[h][:, :, :], part[h][:, 0, :, :], part[h][:, 1, :, :], ALU.add)\
                    .then_inc(gate_ready, 1)
            for h in range(HALVES):
                dve.wait_ge(B2_ps, h + 1)
                if h == 0:
                    dve.wait_ge(consts_ready, 4)
                nc.vector.tensor_tensor(acc[h][:, :, 0, :], T[h][:, :, :], ps_B2[h], ALU.add)\
                    .then_inc(acc_ready, 1)
            rest_w1(2)
            rest_w1(3)

            def gated_sum(s):
                h, e = s // E, s % E
                dve.wait_ge(layer2_done, J * (s + 1))
                if e > 0:
                    dve.wait_ge(y_used, s)
                else:
                    dve.wait_ge(acc_ready, h + 1)
                for t in range(TILES):
                    a = acc[h][:, t, :, :].rearrange("p k c -> p (k c)")
                    last = nc.vector.scalar_tensor_tensor(out=a, in0=ps_y[s % 2][:, t, :],
                                                          scalar=gate[h][:, t, e:e + 1], in1=a,
                                                          op0=ALU.mult, op1=ALU.add)
                last.then_inc(y_used, 1)
                if e == E - 1:
                    dve.wait_ge(y_used, s + 1)
                    nc.vector.tensor_tensor(fin[h][:, :, :], acc[h][:, :, 0, :], acc[h][:, :, 1, :], ALU.add)\
                        .then_inc(fin_ready, 1)

            for g in range(HALVES * UNITS):
                r = g % RING
                if not (cast_on_act(g) and sub_on_pool(g)):
                    dve.wait_ge(h32_ready, g + 1)
                if not cast_on_act(g):
                    nc.vector.tensor_copy(HH[:, r, :], H32[:, r, :]).then_inc(hh_dve, 1)
                if not sub_on_pool(g):
                    wait_hh(dve, g)
                    if g >= RING:
                        dve.wait_ge(layer2_done, g - RING + 1)
                    nc.vector.tensor_tensor(HL[:, r, :], H32[:, r, :], HH[:, r, :], ALU.subtract)\
                        .then_inc(hl_dve, 1)
                if g > LAG + 1 and (g - LAG) % J == J - 1:
                    gated_sum((g - LAG) // J - 1)
            for s in range((HALVES * UNITS - LAG) // J - 1, HALVES * E):
                gated_sum(s)

        @block.tensor
        def _(pe):
            pe.wait_ge(consts_ready, 1)
            for h in range(HALVES):
                pe.wait_ge(x_in[h], 16)
                for t in range(TILES):
                    last = nc.tensor.transpose(ps_xT[h][:, t, :], X[:, IMG * h + t // PT, P * (t % PT):P * (t % PT) + P],
                                               ident[0:C, 0:C])
                last.then_inc(xT_ps, 1)
            pe.wait_ge(qkv_in, 16 * 6)
            nc.tensor.matmul(ps_AT, WkA[:, :], WqA[:, :], start=True, stop=True).then_inc(AT_ps, 1)
            nc.tensor.transpose(ps_WvT, WvA[:, :], ident[0:C, 0:C]).then_inc(WvT_ps, 1)
            pe.wait_ge(ffn_in, 16 * FFN_LOADS)
            nc.tensor.transpose(ps_gb, GB[:, :], ident[0:2 * E, 0:2 * E]).then_inc(gT_ps, 1)
            for h in range(HALVES):
                pe.wait_ge(xnT_ready, h + 1)
                for t in range(TILES):
                    last = nc.tensor.transpose(ps_xn[h][0:CA, P * t:P * t + P], XnT[h][:, t, :], ident[:, :])
                last.then_inc(xn_ps, 1)
            pe.wait_ge(AT_ready, 1)
            pe.wait_ge(WvT_ready, 1)
            pe.wait_ge(gT_ready, 1)
            for h in range(HALVES):
                pe.wait_ge(xn_ready, h + 1)
                nc.tensor.matmul(ps_G[h][0:CA, :], AT[:, :], XN[h][:, :], start=True, stop=True).then_inc(G_ps, 1)
                for t in range(TILES):
                    last = nc.tensor.matmul(ps_V[h][:, t, :], XN[h][:, P * t:P * t + P], WvT[:, :],
                                            start=True, stop=True)
                last.then_inc(V_ps, 1)
            for h in range(HALVES):
                pe.wait_ge(G_ready, h + 1)
                pe.wait_ge(xT_copied, h + 1)
                for i in range(IMG):
                    for t in range(PT):
                        k = PT * i + t
                        last = nc.tensor.matmul(ps_S[h][i][:, t, :], XN[h][:, P * k:P * k + P],
                                                GS[h][:, PIX * i:PIX * i + PIX], start=True, stop=True)
                    last.then_inc(S_ps, 1)
            for h in range(HALVES):
                pe.wait_ge(V_ready, h + 1)
                for i in range(IMG):
                    pe.wait_ge(prob_ready, IMG * h + i + 1)
                    for t in range(PT):
                        for m in range(PT):
                            c = PIX * m + P * t
                            last = nc.tensor.transpose(ps_PT[h][i][:, c:c + P], PR[h][:, PT * i + t, P * m:P * m + P],
                                                       ident[:, :])
                    last.then_inc(PT_ps, 1)
            for h in range(HALVES):
                for i in range(IMG):
                    if i == 0:
                        pe.wait_ge(PT_act, h + 1)
                    else:
                        pe.wait_ge(PT_dve, h + 1)
                    for t in range(PT):
                        for m in range(PT):
                            last = nc.tensor.matmul(ps_O[h][:, PT * i + t, 0:CA], PTs[h][:, i, m, P * t:P * t + P],
                                                    VT[h][:, PT * i + m, :], start=(m == 0), stop=(m == PT - 1))
                last.then_inc(O_ps, 1)
            for h in range(HALVES):
                pe.wait_ge(x2_ready, h + 1)
                for t in range(TILES):
                    last = nc.tensor.transpose(ps_F[h][:, P * t:P * t + P],
                                               X2[h][:, t, :, :].rearrange("p k c -> p (k c)"), ident[:, :])
                last.then_inc(F_ps, 1)
            for q in range(E // 2):
                pe.wait_ge(w1_in[q], 32)
            for e in range(E):
                for j in range(J):
                    nc.tensor.matmul(ps_b1[:, 0, j, e:e + 1], W1F[0:C, e, :].rearrange("p (m j) -> p j m", j=J)[:, j, :],
                                     gT[0:C, E + e:E + e + 1], start=True, stop=True)
            for j in range(J):
                last = nc.tensor.transpose(ps_b1[:, 1, j, :], b1R[:, :].rearrange("e (m j) -> e j m", j=J)[:, j, :],
                                           ident[0:E, 0:E])
            last.then_inc(b1_ps, 1)
            for h in range(HALVES):
                pe.wait_ge(XL_ready, h + 1)
                if h == 0:
                    pe.wait_ge(Wr_ready, 1)
                for t in range(TILES):
                    nc.tensor.matmul(ps_L[h][:, t, :], XH[h][:, P * t:P * t + P], WrS[:, :], start=True, stop=False)
                    last = nc.tensor.matmul(ps_L[h][:, t, :], XL[h][:, P * t:P * t + P], WrS[:, :],
                                            start=False, stop=True)
                last.then_inc(L_ps, 1)
            pe.wait_ge(b1_ready, 1)
            for h in range(HALVES):
                pe.wait_ge(gate_ready, h + 1)
                for t in range(TILES):
                    last = nc.tensor.transpose(ps_wT[h][0:E, P * t:P * t + P], gate[h][:, t, :], ident[:, :])
                last.then_inc(wT_ps, 1)
            pe.wait_ge(b2_ready, 1)
            for h in range(HALVES):
                pe.wait_ge(gateT_ready, h + 1)
                for t in range(TILES):
                    last = nc.tensor.matmul(ps_B2[h][:, t, :], gateT[h][:, P * t:P * t + P], b2S[:, :],
                                            start=True, stop=True)
                last.then_inc(B2_ps, 1)

            def layer1(g):
                h, e, j = g // UNITS, (g % UNITS) // J, g % J
                pe.wait_ge(W1_ready, e // 2 + 1)
                if g >= 2:
                    pe.wait_ge(h32_ready, g - 1)
                nc.tensor.matmul(ps_z[g % 2], W1S[:, e, j, :], XH[h][:, :], start=True, stop=False)
                nc.tensor.matmul(ps_z[g % 2], W1S[:, e, j, :], XL[h][:, :], start=False, stop=True)\
                    .then_inc(z_ready, 1)

            def layer2(g):
                e, j, s = (g % UNITS) // J, g % J, g // J
                if j == 0 and s >= 2:
                    pe.wait_ge(y_used, s - 1)
                wait_hh(pe, g)
                wait_hl(pe, g)
                for t in range(TILES):
                    hh = HH[:, g % RING, P * t:P * t + P]
                    hl = HL[:, g % RING, P * t:P * t + P]
                    nc.tensor.matmul(ps_y[s % 2][:, t, :], hh, W2S[:, e, j, :, :],
                                     start=(j == 0 and t == 0), stop=False, skip_group_check=True)
                    last = nc.tensor.matmul(ps_y[s % 2][:, t, 0:C], hl, W2S[:, e, j, 0, :],
                                            start=False, stop=(j == J - 1), skip_group_check=True)
                last.then_inc(layer2_done, 1)

            def final(h):
                pe.wait_ge(fin_ready, h + 1)
                for t in range(TILES):
                    last = nc.tensor.transpose(ps_out[h][0:C, P * t:P * t + P], fin[h][:, t, :], ident[:, :])
                last.then_inc(out_ps, 1)

            pe.wait_ge(W2_ready, 1)
            pe.wait_ge(acc_ready, HALVES)
            for g in range(HALVES * UNITS + LAG):
                if g < HALVES * UNITS:
                    layer1(g)
                if g >= LAG:
                    layer2(g - LAG)
                if g == UNITS + LAG + 4:
                    final(0)
            final(1)


_INS = ['x', 'L0_conv_wq', 'L0_conv_bq', 'L0_conv_wk', 'L0_conv_bk', 'L0_conv_wv', 'L0_conv_bv',
        'L0_ffn_Wr', 'L0_ffn_br', 'L0_ffn_ln_g', 'L0_ffn_ln_b', 'L0_ffn_W1', 'L0_ffn_b1', 'L0_ffn_W2',
        'L0_ffn_b2']
_OUTS = [((4, 64, 16, 16), 'float32')]


def kernel(**inputs):
    import numpy as _np
    import concourse.bacc as _bacc
    from concourse import mybir as _mybir
    from concourse.bass_utils import run_bass_kernel_spmd as _run

    nc = _bacc.Bacc("TRN2", target_bir_lowering=False, num_devices=1)
    arrays, args = {}, []
    for name in _INS:
        a = _np.ascontiguousarray(inputs[name])
        arrays[f"in_{name}_dram"] = a
        args.append(nc.dram_tensor(f"in_{name}_dram", a.shape, _mybir.dt.from_np(a.dtype), kind="ExternalInput").ap())
    for i, (shape, dtype) in enumerate(_OUTS):
        dt = _mybir.dt.from_np(_np.dtype(dtype))
        args.append(nc.dram_tensor(f"out_{i}_dram", shape, dt, kind="ExternalOutput").ap())
    build_block(nc, *args)
    r = _run(nc, [arrays], core_ids=[0])
    got = tuple(r.results[0][f"out_{i}_dram"] for i in range(len(_OUTS)))
    return got[0]
```

```python
from contextlib import ExitStack

import concourse.bass as bass
from concourse import mybir

F32 = mybir.dt.float32
F16 = mybir.dt.float16
U32 = mybir.dt.uint32
ALU = mybir.AluOpType
ACT = mybir.ActivationFunctionType
AX_X = mybir.AxisListType.X

P = 128
IMAGES, C, PIX = 4, 64, 256
D = 16
E, HID = 8, 256
HALVES = 2
IMG = IMAGES // HALVES
TOK = IMG * PIX
TILES = TOK // P
PT = PIX // P
J = HID // P
UNITS = E * J
CA = C + 1
DB = 32
QK = 3 * DB
EPS_C, EPS_T = 1e-6, 1e-5
SX = 2.0 ** 8
SW = 2.0 ** 8
SG = 2.0 ** -8
RING = 8

A_WQ, A_WK, A_WV, A_WR, A_BV, A_BQ, A_BK, A_END = 0, QK, 2 * QK, 2 * QK + C, 2 * QK + C + E, \
    2 * QK + 2 * C + E, 2 * QK + 2 * C + E + 1, 2 * QK + 2 * C + E + 2
F_G, F_B, F_B1, F_BR, F_B2, F_END = 0, E, 2 * E, 2 * E + UNITS, 3 * E + UNITS, 3 * E + UNITS + C

LAG = 5


def cast_on_act(g):
    return g % 5 in (0, 2)


def sub_on_pool(g):
    return g % 3 == 1


def count(which, g):
    return sum(1 for i in range(g + 1) if which(i))


def build_block(nc, x, attn_w, ffn_w, w1, w2, out):
    with ExitStack() as ctx:
        def sb(name, shape, dt=F32):
            return ctx.enter_context(nc.sbuf_tensor(name, shape, dt))

        def sem(name):
            return ctx.enter_context(nc.semaphore(name))

        banks = ctx.enter_context(nc.psum_tensor("banks", [P, 8, 512], F32))
        BK = [[banks[:, 4 * h + i, :] for i in range(4)] for h in range(HALVES)]
        ps_xn = [BK[h][1] for h in range(HALVES)]
        ps_q = [BK[h][2] for h in range(HALVES)]
        ps_k = [BK[h][3] for h in range(HALVES)]
        ps_V = [BK[h][0][:, 0:TILES * C].rearrange("p (t c) -> p t c", t=TILES) for h in range(HALVES)]
        ps_S = [[BK[h][1 - i].rearrange("p (t m) -> p t m", t=PT) for i in range(IMG)] for h in range(HALVES)]
        ps_PT = [[BK[h][2 + i] for i in range(IMG)] for h in range(HALVES)]
        ps_O = [BK[h][1].rearrange("p (t c) -> p t c", t=TILES) for h in range(HALVES)]
        ps_F = [BK[h][0] for h in range(HALVES)]
        ps_L = [BK[h][2][:, 0:TILES * E].rearrange("p (t e) -> p t e", t=TILES) for h in range(HALVES)]
        ps_wT = [BK[h][3] for h in range(HALVES)]
        ps_B2 = [BK[h][2][:, 0:TILES * C].rearrange("p (t c) -> p t c", t=TILES) for h in range(HALVES)]
        ps_z = [BK[0][1], BK[0][0]]
        ps_y = [BK[0][2 + i][:, 0:TILES * C].rearrange("p (t c) -> p t c", t=TILES) for i in range(2)]
        ps_b1 = BK[1][0][:, 0:UNITS]

        X = sb("X", [P, IMAGES * PT, C])
        PA = sb("PA", [P, A_END])
        PF = sb("PF", [P, F_END])
        WA = sb("WA", [P, A_BV], F16)
        gS = sb("gS", [P, E])
        b1S = sb("b1S", [P, UNITS])
        b2S = sb("b2S", [E, C])
        W1F = sb("W1F", [P, E, J, P])
        W1G = sb("W1G", [P, E, J, P])
        W1S = sb("W1S", [P, E, J, P], F16)
        W2F = sb("W2F", [P, UNITS, C])
        W2S = sb("W2S", [P, 2, UNITS, C], F16)
        ident = sb("ident", [P, P])
        iota = sb("iota", [P, E])
        half = sb("half", [P, TILES])

        def both(name, shape, dt=F32):
            return [sb(f"{name}{h}", shape, dt) for h in range(HALVES)]

        st = both("st", [P, TILES, 6])
        mv = both("mv", [P, TILES, 2])
        base1 = both("base1", [P, TILES])
        rs1 = both("rs1", [P, TILES])
        rs1s = both("rs1s", [P, TILES])
        X1 = both("X1", [P, TILES, 2, C])
        X1H = both("X1H", [P, TOK], F16)
        X1L = both("X1L", [P, TOK], F16)
        Q32 = both("Q32", [QK, TOK])
        K32 = both("K32", [QK, TOK])
        QS = both("QS", [QK, TOK], F16)
        KS = both("KS", [QK, TOK], F16)
        V32 = both("V32", [P, TILES, C])
        VH = both("VH", [P, TILES, CA], F16)
        VL = both("VL", [P, TILES, CA], F16)
        nmax = both("nmax", [P, TILES])
        PR = both("PR", [P, TILES, PIX])
        PTH = both("PTH", [P, IMG, PT, PIX], F16)
        PTL = both("PTL", [P, IMG, PT, PIX], F16)
        rsum = both("rsum", [P, TILES])
        T = both("T", [P, TILES, C])
        st2 = both("st2", [P, TILES, 6])
        mv2 = both("mv2", [P, TILES, 2])
        base2 = both("base2", [P, 2, TILES])
        rs2 = both("rs2", [P, 2, TILES])
        rs2s = both("rs2s", [P, TILES])
        X2 = both("X2", [P, TILES, 2, C])
        XH = both("XH", [P, TOK], F16)
        XL = both("XL", [P, TOK], F16)
        inv2 = both("inv2", [P, TILES])
        ratio = both("ratio", [P, TILES])
        LG = both("LG", [P, TILES, E])
        top = both("top", [P, TILES, 8])
        topi = both("topi", [P, TILES, 8], U32)
        topf = both("topf", [P, TILES, 2])
        gap = both("gap", [P, TILES])
        th = both("th", [P, TILES])
        wab = both("wab", [P, 2, TILES])
        hot = both("hot", [P, 2, TILES, E])
        gate = both("gate", [P, TILES, E])
        part = both("part", [P, 2, TILES, E])
        gateT = both("gateT", [E, TOK])
        acc = both("acc", [P, TILES, C])
        gated = sb("gated", [P, 2, TILES, C])
        H32 = sb("H32", [P, RING, TOK])
        HH = sb("HH", [P, RING, TOK], F16)
        HL = sb("HL", [P, RING, TOK], F16)

        x_in = [sem(f"x_in{h}") for h in range(HALVES)]
        attn_in = sem("attn_in")
        ffn_in = sem("ffn_in")
        w1_in = [sem(f"w1_in{i}") for i in range(2)]
        w2_in = sem("w2_in")
        out_done = [sem(f"out_done{h}") for h in range(HALVES)]
        pool_step = sem("pool_step")
        ident_ready = sem("ident_ready")
        half_ready = sem("half_ready")
        ones_ready = sem("ones_ready")
        iota_ready = sem("iota_ready")
        vec_step = sem("vec_step")
        WA_hi = sem("WA_hi")
        WA_ready = sem("WA_ready")
        gS_ready = sem("gS_ready")
        b1_ps = sem("b1_ps")
        b1_ready = sem("b1_ready")
        b2_ready = sem("b2_ready")
        W1_scaled = sem("W1_scaled")
        W1_hi = sem("W1_hi")
        W1_ready = sem("W1_ready")
        W2_hi = sem("W2_hi")
        W2_ready = sem("W2_ready")
        var1_ready = sem("var1_ready")
        rs1_ready = sem("rs1_ready")
        x1_ready = sem("x1_ready")
        xn_ps = sem("xn_ps")
        X1H_ready = sem("X1H_ready")
        X1L_ready = sem("X1L_ready")
        q_ps = sem("q_ps")
        k_ps = sem("k_ps")
        V_ps = sem("V_ps")
        q32_ready = sem("q32_ready")
        k32_ready = sem("k32_ready")
        q_hi = sem("q_hi")
        k_hi = sem("k_hi")
        q_ready = sem("q_ready")
        k_ready = sem("k_ready")
        V_hi = sem("V_hi")
        V_ready = sem("V_ready")
        S_ps = sem("S_ps")
        nmax_ready = sem("nmax_ready")
        prob_ready = sem("prob_ready")
        PT_ps = sem("PT_ps")
        PT_hi = sem("PT_hi")
        PT_ready = sem("PT_ready")
        O_ps = sem("O_ps")
        var2_ready = sem("var2_ready")
        rs2_ready = sem("rs2_ready")
        rs2b_ready = sem("rs2b_ready")
        x2_ready = sem("x2_ready")
        F_ps = sem("F_ps")
        XH_ready = sem("XH_ready")
        XL_ready = sem("XL_ready")
        L_ps = sem("L_ps")
        gap_ready = sem("gap_ready")
        th_ready = sem("th_ready")
        gate_ready = sem("gate_ready")
        wT_ps = sem("wT_ps")
        gateT_ready = sem("gateT_ready")
        B2_ps = sem("B2_ps")
        acc_ready = sem("acc_ready")
        z_ready = sem("z_ready")
        h32_ready = sem("h32_ready")
        hh_act = sem("hh_act")
        hh_dve = sem("hh_dve")
        hl_pool = sem("hl_pool")
        hl_dve = sem("hl_dve")
        layer2_done = sem("layer2_done")
        y_used = sem("y_used")
        summed = sem("summed")

        block = ctx.enter_context(nc.Block())

        def wait_hh(eng, g):
            if cast_on_act(g):
                eng.wait_ge(hh_act, count(cast_on_act, g))
            else:
                eng.wait_ge(hh_dve, g + 1 - count(cast_on_act, g))

        def wait_hl(eng, g):
            if sub_on_pool(g):
                eng.wait_ge(hl_pool, count(sub_on_pool, g))
            else:
                eng.wait_ge(hl_dve, g + 1 - count(sub_on_pool, g))

        @block.sync
        def _(sp):
            sp.dma_start(X[:, 0:TILES, :], x[:, 0:TILES, :]).then_inc(x_in[0], 16)
            sp.dma_start(X[:, TILES:2 * TILES, :], x[:, TILES:2 * TILES, :]).then_inc(x_in[1], 16)
            sp.dma_start(PA[:, :], attn_w).then_inc(attn_in, 16)
            sp.dma_start(PF[:, :], ffn_w).then_inc(ffn_in, 16)
            sp.dma_start(W1F[:, 0:2, :, :], w1[:, 0:2, :, :]).then_inc(w1_in[0], 16)
            sp.dma_start(W2F[:, :, :], w2).then_inc(w2_in, 16)
            sp.dma_start(W1F[:, 2:E, :, :], w1[:, 2:E, :, :]).then_inc(w1_in[1], 16)
            for h in range(HALVES):
                sp.wait_ge(summed, E * (h + 1))
                sp.dma_start(out[:, TILES * h:TILES * h + TILES, :], acc[h][:, :, :]).then_inc(out_done[h], 16)
            for h in range(HALVES):
                sp.wait_ge(out_done[h], 16)

        @block.gpsimd
        def _(pool):
            nc.gpsimd.memset(half[:, :], -0.5).then_inc(half_ready, 1)
            nc.gpsimd.memset(ident[:, :], 0.0).then_inc(pool_step, 1)
            pool.wait_ge(pool_step, 1)
            nc.gpsimd.affine_select(out=ident[:, :], in_=ident[:, :], compare_op=ALU.not_equal, fill=1.0,
                                    base=0, pattern=[[-1, P]], channel_multiplier=1)\
                .then_inc(ident_ready, 1)
            for h in range(HALVES):
                nc.gpsimd.memset(VH[h][:, :, C:CA], 1.0)
                last = nc.gpsimd.memset(VL[h][:, :, C:CA], 0.0)
            last.then_inc(ones_ready, 1)
            for h in range(HALVES):
                pool.wait_ge(var1_ready, h + 1)
                pool.wait_ge(half_ready, 1)
                nc.gpsimd.tensor_tensor(rs1[h][:, :], base1[h][:, :], half[:, :], ALU.pow)\
                    .then_inc(rs1_ready, 1)
            for e in range(E):
                last = nc.gpsimd.memset(iota[:, e:e + 1], float(e))
            last.then_inc(iota_ready, 1)

            def scale_w1(q):
                pool.wait_ge(w1_in[min(q, 1)], 16)
                pool.wait_ge(gS_ready, 1)
                es = slice(2 * q, 2 * q + 2)
                nc.gpsimd.tensor_tensor(W1G[:, es, :, :].rearrange("p e j m -> p e (j m)"),
                                        W1F[:, es, :, :].rearrange("p e j m -> p e (j m)"),
                                        gS[:, es].unsqueeze(2).broadcast_to([P, 2, HID]),
                                        ALU.mult).then_inc(W1_scaled, 1)

            scale_w1(0)
            for h in range(HALVES):
                pool.wait_ge(q_hi, h + 1)
                pool.wait_ge(W1_scaled, 1)
                if h >= 1:
                    pool.wait_ge(k_ready, h)
                nc.gpsimd.tensor_tensor(QS[h][DB:2 * DB, :], Q32[h][DB:2 * DB, :], QS[h][DB:2 * DB, :],
                                        ALU.subtract).then_inc(q_ready, 1)
                pool.wait_ge(k_hi, h + 1)
                pool.wait_ge(q_ready, h + 1)
                nc.gpsimd.tensor_tensor(KS[h][2 * DB:QK, :], K32[h][2 * DB:QK, :], KS[h][2 * DB:QK, :],
                                        ALU.subtract).then_inc(k_ready, 1)
            for h in range(HALVES):
                pool.wait_ge(V_hi, h + 1)
                if h == 0:
                    pool.wait_ge(k_ready, HALVES)
                nc.gpsimd.tensor_tensor(VL[h][:, :, 0:C], V32[h][:, :, :], VH[h][:, :, 0:C],
                                        ALU.subtract).then_inc(V_ready, 1)
            scale_w1(1)
            for h in range(HALVES):
                pool.wait_ge(var2_ready, h + 1)
                nc.gpsimd.tensor_tensor(rs2[h][:, 0, :], base2[h][:, 0, :], half[:, :], ALU.pow)\
                    .then_inc(rs2_ready, 1)
                nc.gpsimd.tensor_tensor(rs2[h][:, 1, :], base2[h][:, 1, :], half[:, :], ALU.pow)\
                    .then_inc(rs2b_ready, 1)
            scale_w1(2)
            scale_w1(3)

            def sum_y(s):
                h = s // E
                pool.wait_ge(y_used, s + 1)
                if s % E == 0:
                    pool.wait_ge(acc_ready, h + 1)
                else:
                    pool.wait_ge(summed, s)
                nc.gpsimd.tensor_tensor(acc[h][:, :, :], acc[h][:, :, :], gated[:, s % 2, :, :], ALU.add)\
                    .then_inc(summed, 1)

            for g in range(HALVES * UNITS):
                if sub_on_pool(g):
                    r = g % RING
                    pool.wait_ge(h32_ready, g + 1)
                    wait_hh(pool, g)
                    if g >= RING:
                        pool.wait_ge(layer2_done, g - RING + 1)
                    nc.gpsimd.tensor_tensor(HL[:, r, :], H32[:, r, :], HH[:, r, :], ALU.subtract)\
                        .then_inc(hl_pool, 1)
                if g > LAG + 1 and (g - LAG) % J == J - 1:
                    sum_y((g - LAG) // J - 1)
            for s in range((HALVES * UNITS - LAG) // J - 1, HALVES * E):
                sum_y(s)

        @block.scalar
        def _(act):
            act.wait_ge(attn_in, 16)
            nc.scalar.mul(WA[:, :], PA[:, 0:A_BV], SW).then_inc(WA_hi, 1)
            for h in range(HALVES):
                act.wait_ge(xn_ps, h + 1)
                nc.scalar.copy(X1H[h][:, :], ps_xn[h]).then_inc(X1H_ready, 1)
            for h in range(HALVES):
                act.wait_ge(q_ps, h + 1)
                nc.scalar.activation(Q32[h][:, :], ps_q[h][0:QK, :], ACT.Identity, scale=1.0 / (SX * SW),
                                     bias=PA[0:QK, A_BQ:A_BQ + 1]).then_inc(q32_ready, 1)
                act.wait_ge(k_ps, h + 1)
                nc.scalar.activation(K32[h][:, :], ps_k[h][0:QK, :], ACT.Identity, scale=1.0 / (SX * SW),
                                     bias=PA[0:QK, A_BK:A_BK + 1]).then_inc(k32_ready, 1)

            def split_w1(q):
                act.wait_ge(W1_scaled, q + 1)
                nc.scalar.copy(W1S[:, 2 * q:2 * q + 2, :, :], W1G[:, 2 * q:2 * q + 2, :, :]).then_inc(W1_hi, 1)

            split_w1(0)
            for h in range(HALVES):
                for i in range(IMG):
                    act.wait_ge(nmax_ready, IMG * h + i + 1)
                    for t in range(PT):
                        k = PT * i + t
                        last = nc.scalar.activation(PR[h][:, k, :], ps_S[h][i][:, t, :], ACT.Exp,
                                                    bias=nmax[h][:, k:k + 1])
                    last.then_inc(prob_ready, 1)
            for h in range(HALVES):
                for i in range(IMG):
                    act.wait_ge(PT_ps, IMG * h + i + 1)
                    nc.scalar.copy(PTH[h][:, i, :, :], ps_PT[h][i].rearrange("p (t n) -> p t n", t=PT))\
                        .then_inc(PT_hi, 1)
            act.wait_ge(w2_in, 16)
            nc.scalar.mul(W2S[:, 0, :, :], W2F[:, :, :], SW).then_inc(W2_hi, 1)
            split_w1(1)
            for h in range(HALVES):
                act.wait_ge(F_ps, h + 1)
                nc.scalar.copy(XH[h][:, :], ps_F[h]).then_inc(XH_ready, 1)
            for h in range(HALVES):
                act.wait_ge(gap_ready, h + 1)
                nc.scalar.activation(th[h][:, :], gap[h][:, :], ACT.Tanh, scale=0.5).then_inc(th_ready, 1)
                act.wait_ge(wT_ps, h + 1)
                nc.scalar.copy(gateT[h][:, :], ps_wT[h][0:E, :]).then_inc(gateT_ready, 1)
            split_w1(2)
            split_w1(3)
            act.wait_ge(b1_ready, 1)
            for g in range(HALVES * UNITS):
                u, r = g % UNITS, g % RING
                act.wait_ge(z_ready, g + 1)
                if g >= RING:
                    wait_hl(act, g - RING)
                    act.wait_ge(layer2_done, g - RING + 1)
                if cast_on_act(g):
                    nc.scalar.activation(HH[:, r, :], ps_z[g % 2], ACT.Gelu, bias=b1S[:, u:u + 1],
                                         scale=1.0 / (SX * SW)).then_inc(hh_act, 1)
                nc.scalar.activation(H32[:, r, :], ps_z[g % 2], ACT.Gelu, bias=b1S[:, u:u + 1],
                                     scale=1.0 / (SX * SW)).then_inc(h32_ready, 1)

        @block.vector
        def _(dve):
            chain = [0]

            def step(ins):
                chain[0] += 1
                ins.then_inc(vec_step, 1)
                dve.wait_ge(vec_step, chain[0])

            def stats(src, s6, m2):
                for t in range(TILES):
                    last = nc.vector.bn_stats(s6[:, t, :], src[:, t, :])
                step(last)
                for t in range(TILES):
                    last = nc.vector.bn_aggr(m2[:, t, :], s6[:, t, :])
                step(last)

            for h in range(HALVES):
                dve.wait_ge(x_in[h], 16)
                stats(X[:, TILES * h:TILES * h + TILES, :], st[h], mv[h])
                nc.vector.tensor_scalar(base1[h][:, :], mv[h][:, :, 1], EPS_C, None, ALU.add)\
                    .then_inc(var1_ready, 1)
            dve.wait_ge(WA_hi, 1)
            nc.vector.scalar_tensor_tensor(out=WA[C:P, :], in0=PA[C:P, 0:A_BV], scalar=SW, in1=WA[C:P, :],
                                           op0=ALU.mult, op1=ALU.subtract).then_inc(WA_ready, 1)
            for h in range(HALVES):
                dve.wait_ge(rs1_ready, h + 1)
                step(nc.vector.tensor_scalar(rs1s[h][:, :], rs1[h][:, :], SX, None, ALU.mult))
                for t in range(TILES):
                    last = nc.vector.tensor_scalar(X1[h][:, t, :, :],
                                                   X[:, TILES * h + t, :].unsqueeze(1).broadcast_to([P, 2, C]),
                                                   mv[h][:, t, 0:1], rs1s[h][:, t:t + 1],
                                                   ALU.subtract, ALU.mult)
                last.then_inc(x1_ready, 1)
            for h in range(HALVES):
                dve.wait_ge(X1H_ready, h + 1)
                nc.vector.tensor_tensor(X1L[h][:, :], ps_xn[h], X1H[h][:, :], ALU.subtract).then_inc(X1L_ready, 1)
            dve.wait_ge(ffn_in, 16)
            nc.vector.tensor_scalar(gS[:, :], PF[:, F_G:F_G + E], SW, None, ALU.mult).then_inc(gS_ready, 1)
            nc.vector.tensor_scalar(b2S[:, :], PF[0:E, F_B2:F_B2 + C], 1.0 / SG, None, ALU.mult)\
                .then_inc(b2_ready, 1)
            for h in range(HALVES):
                dve.wait_ge(q32_ready, h + 1)
                nc.vector.tensor_copy(QS[h][:, :], Q32[h][:, :]).then_inc(q_hi, 1)
                dve.wait_ge(k32_ready, h + 1)
                nc.vector.tensor_copy(KS[h][:, :], K32[h][:, :]).then_inc(k_hi, 1)
                dve.wait_ge(V_ps, h + 1)
                step(nc.vector.scalar_tensor_tensor(out=V32[h][:, :, :], in0=ps_V[h], scalar=1.0 / (SX * SW),
                                                    in1=PA[:, A_BV:A_BV + C].unsqueeze(1)
                                                    .broadcast_to([P, TILES, C]),
                                                    op0=ALU.mult, op1=ALU.add))
                nc.vector.tensor_copy(VH[h][:, :, 0:C], V32[h][:, :, :]).then_inc(V_hi, 1)
            for h in range(HALVES):
                for i in range(IMG):
                    dve.wait_ge(S_ps, IMG * h + i + 1)
                    nc.vector.tensor_reduce(nmax[h][:, PT * i:PT * i + PT], ps_S[h][i], AX_X, ALU.max,
                                            negate=True).then_inc(nmax_ready, 1)
            for h in range(HALVES):
                for i in range(IMG):
                    dve.wait_ge(PT_hi, IMG * h + i + 1)
                    nc.vector.tensor_tensor(PTL[h][:, i, :, :], ps_PT[h][i].rearrange("p (t n) -> p t n", t=PT),
                                            PTH[h][:, i, :, :], ALU.subtract).then_inc(PT_ready, 1)

            def rest_w1(q):
                dve.wait_ge(W1_hi, q + 1)
                es = slice(2 * q, 2 * q + 2)
                nc.vector.tensor_tensor(W1S[C:P, es, :, :], W1G[C:P, es, :, :], W1S[C:P, es, :, :],
                                        ALU.subtract).then_inc(W1_ready, 1)

            for h in range(HALVES):
                dve.wait_ge(O_ps, h + 1)
                step(nc.vector.reciprocal(rsum[h][:, :], ps_O[h][:, :, C]))
                for t in range(TILES):
                    last = nc.vector.scalar_tensor_tensor(out=T[h][:, t, :], in0=ps_O[h][:, t, 0:C],
                                                          scalar=rsum[h][:, t:t + 1], in1=X[:, TILES * h + t, :],
                                                          op0=ALU.mult, op1=ALU.add)
                step(last)
                stats(T[h], st2[h], mv2[h])
                nc.vector.tensor_scalar(base2[h][:, 0, :], mv2[h][:, :, 1], 1.0 + EPS_T, EPS_T * EPS_T,
                                        ALU.mult, ALU.add)
                nc.vector.tensor_scalar(base2[h][:, 1, :], mv2[h][:, :, 1], EPS_T, None, ALU.add)\
                    .then_inc(var2_ready, 1)
            dve.wait_ge(b1_ps, 1)
            nc.vector.tensor_tensor(b1S[:, :], ps_b1, PF[:, F_B1:F_B1 + UNITS], ALU.add).then_inc(b1_ready, 1)
            rest_w1(0)
            for h in range(HALVES):
                dve.wait_ge(rs2_ready, h + 1)
                step(nc.vector.tensor_scalar(rs2s[h][:, :], rs2[h][:, 0, :], SX, None, ALU.mult))
                for t in range(TILES):
                    last = nc.vector.tensor_scalar(X2[h][:, t, :, :],
                                                   T[h][:, t, :].unsqueeze(1).broadcast_to([P, 2, C]),
                                                   mv2[h][:, t, 0:1],
                                                   rs2s[h][:, t:t + 1], ALU.subtract, ALU.mult)
                last.then_inc(x2_ready, 1)
            dve.wait_ge(W2_hi, 1)
            nc.vector.scalar_tensor_tensor(out=W2S[:, 1, :, :], in0=W2F[:, :, :], scalar=SW,
                                           in1=W2S[:, 0, :, :], op0=ALU.mult, op1=ALU.subtract)\
                .then_inc(W2_ready, 1)
            for h in range(HALVES):
                dve.wait_ge(XH_ready, h + 1)
                nc.vector.tensor_tensor(XL[h][:, :], ps_F[h], XH[h][:, :], ALU.subtract).then_inc(XL_ready, 1)
            rest_w1(1)
            for h in range(HALVES):
                dve.wait_ge(rs2b_ready, h + 1)
                step(nc.vector.reciprocal(inv2[h][:, :], rs2s[h][:, :]))
                step(nc.vector.scalar_tensor_tensor(out=ratio[h][:, :], in0=rs2[h][:, 1, :], scalar=1.0 / SW,
                                                    in1=inv2[h][:, :], op0=ALU.mult, op1=ALU.mult))
                dve.wait_ge(L_ps, h + 1)
                for t in range(TILES):
                    last = nc.vector.scalar_tensor_tensor(out=LG[h][:, t, :], in0=ps_L[h][:, t, :],
                                                          scalar=ratio[h][:, t:t + 1], in1=PF[:, F_BR:F_BR + E],
                                                          op0=ALU.mult, op1=ALU.add)
                step(last)
                for t in range(TILES):
                    last = nc.vector.max(top[h][:, t, :], LG[h][:, t, :])
                step(last)
                nc.vector.tensor_tensor(gap[h][:, :], top[h][:, :, 0], top[h][:, :, 1], ALU.subtract)\
                    .then_inc(gap_ready, 1)
                for t in range(TILES):
                    last = nc.vector.max_index(topi[h][:, t, :], top[h][:, t, :], LG[h][:, t, :])
                step(last)
                step(nc.vector.tensor_copy(topf[h][:, :, :], topi[h][:, :, 0:2]))
                dve.wait_ge(iota_ready, 1)
                for k in range(2):
                    last = nc.vector.tensor_tensor(hot[h][:, k, :, :],
                                                   iota[:, :].unsqueeze(1).broadcast_to([P, TILES, E]),
                                                   topf[h][:, :, k:k + 1].broadcast_to([P, TILES, E]),
                                                   ALU.is_equal)
                dve.wait_ge(th_ready, h + 1)
                for k in range(2):
                    last = nc.vector.tensor_scalar(wab[h][:, k, :], th[h][:, :], (0.5 - k) * SG, 0.5 * SG,
                                                   ALU.mult, ALU.add)
                step(last)
                for k in range(2):
                    last = nc.vector.tensor_tensor(part[h][:, k, :, :], hot[h][:, k, :, :],
                                                   wab[h][:, k, :].unsqueeze(2).broadcast_to([P, TILES, E]),
                                                   ALU.mult)
                step(last)
                nc.vector.tensor_tensor(gate[h][:, :, :], part[h][:, 0, :, :], part[h][:, 1, :, :], ALU.add)\
                    .then_inc(gate_ready, 1)
            for h in range(HALVES):
                dve.wait_ge(B2_ps, h + 1)
                nc.vector.tensor_tensor(acc[h][:, :, :], T[h][:, :, :], ps_B2[h], ALU.add)\
                    .then_inc(acc_ready, 1)
            rest_w1(2)
            rest_w1(3)

            def gate_y(s):
                h, e = s // E, s % E
                dve.wait_ge(layer2_done, J * (s + 1))
                if s >= 2:
                    dve.wait_ge(summed, s - 1)
                nc.vector.tensor_tensor(gated[:, s % 2, :, :], ps_y[s % 2],
                                        gate[h][:, :, e:e + 1].broadcast_to([P, TILES, C]), ALU.mult)\
                    .then_inc(y_used, 1)

            for g in range(HALVES * UNITS):
                r = g % RING
                if not (cast_on_act(g) and sub_on_pool(g)):
                    dve.wait_ge(h32_ready, g + 1)
                if not cast_on_act(g):
                    nc.vector.tensor_copy(HH[:, r, :], H32[:, r, :]).then_inc(hh_dve, 1)
                if not sub_on_pool(g):
                    wait_hh(dve, g)
                    if g >= RING:
                        dve.wait_ge(layer2_done, g - RING + 1)
                    nc.vector.tensor_tensor(HL[:, r, :], H32[:, r, :], HH[:, r, :], ALU.subtract)\
                        .then_inc(hl_dve, 1)
                if g > LAG + 1 and (g - LAG) % J == J - 1:
                    gate_y((g - LAG) // J - 1)
            for s in range((HALVES * UNITS - LAG) // J - 1, HALVES * E):
                gate_y(s)

        @block.tensor
        def _(pe):
            pe.wait_ge(ident_ready, 1)
            for h in range(HALVES):
                pe.wait_ge(x1_ready, h + 1)
                for t in range(TILES):
                    last = nc.tensor.transpose(ps_xn[h][:, P * t:P * t + P],
                                               X1[h][:, t, :, :].rearrange("p k c -> p (k c)"), ident[:, :])
                last.then_inc(xn_ps, 1)

            def two_parts(dst, lhsT, part_h, part_l, swap=False):
                for n, part in enumerate((part_h, part_l)):
                    a, b = (part, lhsT) if swap else (lhsT, part)
                    last = nc.tensor.matmul(dst, a, b, start=(n == 0), stop=(n == 1))
                return last

            pe.wait_ge(WA_ready, 1)
            for h in range(HALVES):
                pe.wait_ge(X1L_ready, h + 1)
                two_parts(ps_q[h][0:QK, :], WA[:, A_WQ:A_WQ + QK], X1H[h][:, :], X1L[h][:, :]).then_inc(q_ps, 1)
                two_parts(ps_k[h][0:QK, :], WA[:, A_WK:A_WK + QK], X1H[h][:, :], X1L[h][:, :]).then_inc(k_ps, 1)
                for t in range(TILES):
                    ts = slice(P * t, P * t + P)
                    last = two_parts(ps_V[h][:, t, :], WA[:, A_WV:A_WV + C], X1H[h][:, ts], X1L[h][:, ts], True)
                last.then_inc(V_ps, 1)
            pe.wait_ge(ffn_in, 16)

            def offsets(e):
                for j in range(J):
                    last = nc.tensor.matmul(ps_b1[:, J * e + j:J * e + j + 1], W1F[0:C, e, j, :],
                                            PF[0:C, F_B + e:F_B + e + 1], start=True, stop=True)
                return last

            for h in range(HALVES):
                pe.wait_ge(q_ready, h + 1)
                pe.wait_ge(k_ready, h + 1)
                for i in range(IMG):
                    if i == 1:
                        pe.wait_ge(V_hi, h + 1)
                    for t in range(PT):
                        k = PT * i + t
                        last = nc.tensor.matmul(ps_S[h][i][:, t, :], QS[h][:, P * k:P * k + P],
                                                KS[h][:, PIX * i:PIX * i + PIX], start=True, stop=True)
                    last.then_inc(S_ps, 1)
            for h in range(HALVES):
                for i in range(IMG):
                    pe.wait_ge(prob_ready, IMG * h + i + 1)
                    for t in range(PT):
                        for m in range(PT):
                            c = PIX * m + P * t
                            last = nc.tensor.transpose(ps_PT[h][i][:, c:c + P], PR[h][:, PT * i + t, P * m:P * m + P],
                                                       ident[:, :])
                    last.then_inc(PT_ps, 1)
            pe.wait_ge(ones_ready, 1)
            for h in range(HALVES):
                pe.wait_ge(V_ready, h + 1)
                for i in range(IMG):
                    pe.wait_ge(PT_ready, IMG * h + i + 1)
                    for t in range(PT):
                        k = PT * i + t
                        for m in range(PT):
                            ph = PTH[h][:, i, m, P * t:P * t + P]
                            pl = PTL[h][:, i, m, P * t:P * t + P]
                            vh, vl = VH[h][:, PT * i + m, :], VL[h][:, PT * i + m, :]
                            nc.tensor.matmul(ps_O[h][:, k, 0:CA], ph, vh, start=(m == 0), stop=False)
                            nc.tensor.matmul(ps_O[h][:, k, 0:CA], ph, vl, start=False, stop=False)
                            last = nc.tensor.matmul(ps_O[h][:, k, 0:CA], pl, vh, start=False, stop=(m == PT - 1))
                last.then_inc(O_ps, 1)
            pe.wait_ge(w1_in[0], 16)
            pe.wait_ge(w1_in[1], 16)
            for e in range(E):
                last = offsets(e)
            last.then_inc(b1_ps, 1)
            for h in range(HALVES):
                pe.wait_ge(x2_ready, h + 1)
                if h == 1:
                    pe.wait_ge(b1_ready, 1)
                for t in range(TILES):
                    last = nc.tensor.transpose(ps_F[h][:, P * t:P * t + P],
                                               X2[h][:, t, :, :].rearrange("p k c -> p (k c)"), ident[:, :])
                last.then_inc(F_ps, 1)
            for h in range(HALVES):
                pe.wait_ge(XL_ready, h + 1)
                for t in range(TILES):
                    ts = slice(P * t, P * t + P)
                    last = two_parts(ps_L[h][:, t, :], WA[:, A_WR:A_WR + E], XH[h][:, ts], XL[h][:, ts], True)
                last.then_inc(L_ps, 1)
            for h in range(HALVES):
                pe.wait_ge(gate_ready, h + 1)
                for t in range(TILES):
                    last = nc.tensor.transpose(ps_wT[h][0:E, P * t:P * t + P], gate[h][:, t, :], ident[:, :])
                last.then_inc(wT_ps, 1)
            pe.wait_ge(b2_ready, 1)
            for h in range(HALVES):
                pe.wait_ge(gateT_ready, h + 1)
                for t in range(TILES):
                    last = nc.tensor.matmul(ps_B2[h][:, t, :], gateT[h][:, P * t:P * t + P], b2S[:, :],
                                            start=True, stop=True)
                last.then_inc(B2_ps, 1)

            def layer1(g):
                h, e, j = g // UNITS, (g % UNITS) // J, g % J
                pe.wait_ge(W1_ready, e // 2 + 1)
                if g >= 2:
                    pe.wait_ge(h32_ready, g - 1)
                nc.tensor.matmul(ps_z[g % 2], W1S[:, e, j, :], XH[h][:, :], start=True, stop=False)
                nc.tensor.matmul(ps_z[g % 2], W1S[:, e, j, :], XL[h][:, :], start=False, stop=True)\
                    .then_inc(z_ready, 1)

            def layer2(g):
                u, j, s = g % UNITS, g % J, g // J
                if j == 0 and s >= 2:
                    pe.wait_ge(y_used, s - 1)
                wait_hh(pe, g)
                wait_hl(pe, g)
                for t in range(TILES):
                    hh = HH[:, g % RING, P * t:P * t + P]
                    hl = HL[:, g % RING, P * t:P * t + P]
                    nc.tensor.matmul(ps_y[s % 2][:, t, :], hh, W2S[:, 0, u, :],
                                     start=(j == 0 and t == 0), stop=False, skip_group_check=True)
                    nc.tensor.matmul(ps_y[s % 2][:, t, :], hh, W2S[:, 1, u, :],
                                     start=False, stop=False, skip_group_check=True)
                    last = nc.tensor.matmul(ps_y[s % 2][:, t, :], hl, W2S[:, 0, u, :],
                                            start=False, stop=(j == J - 1), skip_group_check=True)
                last.then_inc(layer2_done, 1)

            pe.wait_ge(W2_ready, 1)
            pe.wait_ge(acc_ready, HALVES)
            for g in range(HALVES * UNITS + LAG):
                if g < HALVES * UNITS:
                    layer1(g)
                if g >= LAG:
                    layer2(g - LAG)


_OUTS = [((P, IMAGES * PT, C), 'float32')]


def laid_out(x, L0_conv_wq, L0_conv_bq, L0_conv_wk, L0_conv_bk, L0_conv_wv, L0_conv_bv, L0_ffn_Wr,
             L0_ffn_br, L0_ffn_ln_g, L0_ffn_ln_b, L0_ffn_W1, L0_ffn_b1, L0_ffn_W2, L0_ffn_b2):
    import numpy as np

    tokens = x.reshape(IMAGES, C, PT, P).transpose(3, 0, 2, 1).reshape(P, IMAGES * PT, C)
    a = np.zeros((P, A_END), np.float32)
    f = np.zeros((P, F_END), np.float32)
    for top in (0, C):
        rows = slice(top, top + C)
        for b in range(3):
            a[rows, A_WQ + DB * b:A_WQ + DB * b + D] = L0_conv_wq.T
            a[rows, A_WK + DB * b:A_WK + DB * b + D] = L0_conv_wk.T
        a[rows, A_WV:A_WV + C] = L0_conv_wv.T
        a[rows, A_WR:A_WR + E] = L0_ffn_Wr
        f[rows, F_G:F_G + E] = L0_ffn_ln_g.T
        f[rows, F_B:F_B + E] = L0_ffn_ln_b.T
    for b in range(3):
        a[DB * b:DB * b + D, A_BQ] = L0_conv_bq
        a[DB * b:DB * b + D, A_BK] = L0_conv_bk
    a[:, A_BV:A_BV + C] = L0_conv_bv
    f[:, F_B1:F_B1 + UNITS] = L0_ffn_b1.reshape(UNITS, P).T
    f[:, F_BR:F_BR + E] = L0_ffn_br
    f[0:E, F_B2:F_B2 + C] = L0_ffn_b2
    w1 = L0_ffn_W1.transpose(1, 0, 2).reshape(1, C, E, J, P)
    w1 = np.concatenate([w1, w1]).reshape(P, E, J, P)
    w2 = L0_ffn_W2.reshape(UNITS, P, C).transpose(1, 0, 2)
    return {"x": tokens, "attn_w": a, "ffn_w": f, "w1": w1, "w2": w2}


def kernel(**inputs):
    import numpy as _np
    import concourse.bacc as _bacc
    from concourse import mybir as _mybir
    from concourse.bass_utils import run_bass_kernel_spmd as _run

    nc = _bacc.Bacc("TRN2", target_bir_lowering=False, num_devices=1)
    arrays, args = {}, []
    for name, a in laid_out(**{k: _np.asarray(v) for k, v in inputs.items()}).items():
        a = _np.ascontiguousarray(a)
        arrays[f"in_{name}_dram"] = a
        args.append(nc.dram_tensor(f"in_{name}_dram", a.shape, _mybir.dt.from_np(a.dtype), kind="ExternalInput").ap())
    for i, (shape, dtype) in enumerate(_OUTS):
        dt = _mybir.dt.from_np(_np.dtype(dtype))
        args.append(nc.dram_tensor(f"out_{i}_dram", shape, dt, kind="ExternalOutput").ap())
    build_block(nc, *args)
    r = _run(nc, [arrays], core_ids=[0])
    got = tuple(r.results[0][f"out_{i}_dram"] for i in range(len(_OUTS)))
    return got[0].reshape(P, IMAGES, PT, C).transpose(1, 3, 2, 0).reshape(IMAGES, C, 16, 16)
```

```python
from contextlib import ExitStack

import concourse.bass as bass
from concourse import mybir

F32 = mybir.dt.float32
F16 = mybir.dt.float16
U32 = mybir.dt.uint32
ALU = mybir.AluOpType
ACT = mybir.ActivationFunctionType
AX_X = mybir.AxisListType.X

P = 128
IMAGES, C, PIX = 4, 64, 256
D = 16
E, HID = 8, 256
HALVES = 2
IMG = IMAGES // HALVES
TOK = IMG * PIX
TILES = TOK // P
PT = PIX // P
J = HID // P
UNITS = E * J
CA = C + 1
DB = 32
QK = 3 * DB
EPS_C, EPS_T = 1e-6, 1e-5
SXA = 2.0 ** 4
SWA = 2.0 ** 4
SS = (SXA * SWA) ** 2
SX = 2.0 ** 8
SW = 2.0 ** 8
SG = 2.0 ** -8
WARM = 12
RING = 9
ZB, YB = 4, 4
GB = 4

A_WQ, A_WK, A_WV, A_WR, A_BV, A_BQ, A_BK, A_END = 0, QK, 2 * QK, 2 * QK + C, 2 * QK + C + E, \
    2 * QK + 2 * C + E, 2 * QK + 2 * C + E + 1, 2 * QK + 2 * C + E + 2
F_G, F_B, F_B1, F_BR, F_END = 0, E, 2 * E, 2 * E + UNITS, 3 * E + UNITS

LAG = 6
SUM_END = 12
CAST_ACT = (1, 4, 6, 8, 12, 14, 16, 18, 20, 22, 24, 29, 30, 31)
SUB_POOL = (0, 1, 4, 5, 6, 8, 9, 11, 15, 17, 19, 22, 25, 28, 31)
GZ = 4
G0, G1 = 14, 26
GLAG = 1


def z_bank(g):
    return g % (ZB if g >= GZ else ZB // 2)


def cast_on_act(g):
    return g in CAST_ACT


def sub_on_pool(g):
    return g in SUB_POOL


def sum_on_pool(s):
    return s < SUM_END


def gated_before(g):
    return max(0, (g - LAG - GLAG) // J)


def count(which, g):
    return sum(1 for i in range(g + 1) if which(i))


def build_block(nc, x, attn_w, ffn_w, w1, w2, b2, out):
    with ExitStack() as ctx:
        def sb(name, shape, dt=F32):
            return ctx.enter_context(nc.sbuf_tensor(name, shape, dt))

        def sem(name):
            return ctx.enter_context(nc.semaphore(name))

        banks = ctx.enter_context(nc.psum_tensor("banks", [P, 8, 512], F32))
        BK = [[banks[:, 4 * h + i, :] for i in range(4)] for h in range(HALVES)]
        ps_xn = [[BK[h][(1, 0)[i]][:, 0:PIX] for i in range(IMG)] for h in range(HALVES)]
        ps_q = [BK[h][2] for h in range(HALVES)]
        ps_k = [BK[h][3] for h in range(HALVES)]
        ps_V = [BK[h][0][:, 0:TILES * C].rearrange("p (t c) -> p t c", t=TILES) for h in range(HALVES)]
        ps_S = [[BK[h][1 + i].rearrange("p (t m) -> p t m", t=PT) for i in range(IMG)] for h in range(HALVES)]
        ps_PT = [[BK[h][(3, 0)[i]] for i in range(IMG)] for h in range(HALVES)]
        ps_O = [BK[h][1].rearrange("p (t c) -> p t c", t=TILES) for h in range(HALVES)]
        ps_b1 = [BK[1][1][:, 0:UNITS // 2], BK[0][2][:, 0:UNITS // 2]]
        ps_F = [[BK[h][(2, 1)[i]][:, 0:PIX] for i in range(IMG)] for h in range(HALVES)]
        ps_L = [BK[h][3][:, 0:TILES * E].rearrange("p (t e) -> p t e", t=TILES) for h in range(HALVES)]
        ps_z = [BK[h][i] for h in range(HALVES) for i in (1, 2)]
        ps_y = [BK[h][i][:, 0:TILES * C].rearrange("p (t c) -> p t c", t=TILES)
                for h in range(HALVES) for i in (0, 3)]

        X = sb("X", [P, IMAGES * PT, C])
        PA = sb("PA", [P, A_END])
        PF = sb("PF", [P, F_END])
        WA = sb("WA", [P, A_BV], F16)
        gS = sb("gS", [P, E])
        b1S = sb("b1S", [P, UNITS])
        B2F = sb("B2F", [C, E, C])
        B2S = sb("B2S", [C, E, C], F16)
        ones = sb("ones", [C, P], F16)
        BA = sb("BA", [QK, 2])
        warm = sb("warm", [1, 1])
        W1F = sb("W1F", [P, E, J, P])
        W1G = sb("W1G", [P, E, J, P])
        W1S = sb("W1S", [P, E, J, P], F16)
        W2F = sb("W2F", [P, UNITS, C])
        W2S = sb("W2S", [P, 2, UNITS, C], F16)
        ident = sb("ident", [P, P])
        iota = sb("iota", [P, E])
        half = sb("half", [P, TILES])
        zeros = sb("zeros", [P, TOK], F16)

        def both(name, shape, dt=F32):
            return [sb(f"{name}{h}", shape, dt) for h in range(HALVES)]

        st = both("st", [P, TILES, 6])
        mv = both("mv", [P, TILES, 2])
        base1 = both("base1", [P, TILES])
        rs1 = both("rs1", [P, TILES])
        XC = both("XC", [P, TILES, C])
        X1 = both("X1", [P, TILES, 2, C])
        X1H = both("X1H", [P, TOK], F16)
        X1L = both("X1L", [P, TOK], F16)
        QS = both("QS", [QK, TOK], F16)
        KS = both("KS", [QK, TOK], F16)
        XV = both("XV", [P, TILES, C])
        VH = both("VH", [P, TILES, CA], F16)
        VL = both("VL", [P, TILES, CA], F16)
        peak = both("peak", [P, TILES])
        nmax = both("nmax", [P, TILES])
        PR = both("PR", [P, TILES, PIX])
        PTH = both("PTH", [P, IMG, PT, PIX], F16)
        PTL = both("PTL", [P, IMG, PT, PIX], F16)
        rsum = both("rsum", [P, TILES])
        T = both("T", [P, TILES, C])
        st2 = both("st2", [P, TILES, 6])
        mv2 = both("mv2", [P, TILES, 2])
        base2 = both("base2", [P, 2, TILES])
        rs2 = both("rs2", [P, 2, TILES])
        TC = both("TC", [P, TILES, C])
        X2 = both("X2", [P, TILES, 2, C])
        XH = both("XH", [P, TOK], F16)
        XL = both("XL", [P, TOK], F16)
        inv2 = both("inv2", [P, TILES])
        ratio = both("ratio", [P, TILES])
        LS = both("LS", [P, TILES, E])
        LG = both("LG", [P, TILES, E])
        top = both("top", [P, TILES, 8])
        topi = both("topi", [P, TILES, 8], U32)
        topf = both("topf", [P, TILES, 2])
        gap = both("gap", [P, TILES])
        th = both("th", [P, TILES])
        wab = both("wab", [P, 2, TILES])
        hot = both("hot", [P, 2, TILES, E])
        gate = both("gate", [P, TILES, E])
        part = both("part", [P, 2, TILES, E])
        acc = both("acc", [P, TILES, C])
        gated = sb("gated", [P, GB, TILES, C])
        H32 = sb("H32", [P, RING, TOK])
        HH = sb("HH", [P, RING, TOK], F16)
        HL = sb("HL", [P, RING, TOK], F16)

        x_in = [sem(f"x_in{h}") for h in range(HALVES)]
        attn_in = sem("attn_in")
        ffn_in = sem("ffn_in")
        w1_in = [sem(f"w1_in{i}") for i in range(2)]
        w2_in = sem("w2_in")
        out_done = [sem(f"out_done{h}") for h in range(HALVES)]
        pool_step = sem("pool_step")
        ident_ready = sem("ident_ready")
        half_ready = sem("half_ready")
        zeros_ready = sem("zeros_ready")
        ones_ready = sem("ones_ready")
        iota_ready = sem("iota_ready")
        vec_step = sem("vec_step")
        WA_hi = sem("WA_hi")
        WA_ready = sem("WA_ready")
        gS_ready = sem("gS_ready")
        b1_ps = sem("b1_ps")
        b1_ready = sem("b1_ready")
        b2_in = sem("b2_in")
        b2_hi = sem("b2_hi")
        b2_ready = sem("b2_ready")
        BA_ready = sem("BA_ready")
        W1_scaled = sem("W1_scaled")
        W1_hi = sem("W1_hi")
        W1_ready = sem("W1_ready")
        W2_hi = sem("W2_hi")
        W2_ready = sem("W2_ready")
        var1_ready = sem("var1_ready")
        rs1_ready = sem("rs1_ready")
        xc_ready = sem("xc_ready")
        t_ready = sem("t_ready")
        st_ready = sem("st_ready")
        mv_ready = sem("mv_ready")
        st2_ready = sem("st2_ready")
        mv2_ready = sem("mv2_ready")
        sums_ready = sem("sums_ready")
        tc_ready = sem("tc_ready")
        x1_ready = sem("x1_ready")
        xn_ps = sem("xn_ps")
        X1H_ready = sem("X1H_ready")
        X1L_ready = sem("X1L_ready")
        q_ps = sem("q_ps")
        k_ps = sem("k_ps")
        V_ps = sem("V_ps")
        q_hi = sem("q_hi")
        k_hi = sem("k_hi")
        q_ready = sem("q_ready")
        k_ready = sem("k_ready")
        V_hi = sem("V_hi")
        V_ready = sem("V_ready")
        S_ps = sem("S_ps")
        peak_ready = sem("peak_ready")
        xv_ready = sem("xv_ready")
        nmax_ready = sem("nmax_ready")
        prob_ready = sem("prob_ready")
        PT_ps = sem("PT_ps")
        PT_hi = sem("PT_hi")
        PT_ready = sem("PT_ready")
        O_ps = sem("O_ps")
        var2_ready = sem("var2_ready")
        rs2_ready = sem("rs2_ready")
        rs2b_ready = sem("rs2b_ready")
        x2_ready = sem("x2_ready")
        F_ps = sem("F_ps")
        XH_ready = sem("XH_ready")
        XL_ready = sem("XL_ready")
        L_ps = sem("L_ps")
        gap_ready = sem("gap_ready")
        th_ready = sem("th_ready")
        gate_ready = sem("gate_ready")
        logits_ready = sem("logits_ready")
        top_ready = sem("top_ready")
        topf_ready = sem("topf_ready")
        wab_ready = sem("wab_ready")
        z_ready = sem("z_ready")
        h32_ready = sem("h32_ready")
        hh_act = sem("hh_act")
        hh_dve = sem("hh_dve")
        hl_pool = sem("hl_pool")
        hl_dve = sem("hl_dve")
        layer2_done = sem("layer2_done")
        y_used = sem("y_used")
        summed = sem("summed")

        block = ctx.enter_context(nc.Block())

        def wait_hh(eng, g):
            if cast_on_act(g):
                eng.wait_ge(hh_act, count(cast_on_act, g))
            else:
                eng.wait_ge(hh_dve, g + 1 - count(cast_on_act, g))

        def wait_hl(eng, g):
            if sub_on_pool(g):
                eng.wait_ge(hl_pool, count(sub_on_pool, g))
            else:
                eng.wait_ge(hl_dve, g + 1 - count(sub_on_pool, g))

        @block.sync
        def _(sp):
            sp.dma_start(X[:, 0:TILES, :], x[:, 0:TILES, :]).then_inc(x_in[0], 16)
            sp.dma_start(B2F[:, :, :], b2).then_inc(b2_in, 16)
            sp.dma_start(X[:, TILES:2 * TILES, :], x[:, TILES:2 * TILES, :]).then_inc(x_in[1], 16)
            sp.dma_start(PF[:, :], ffn_w).then_inc(ffn_in, 16)
            sp.dma_start(W1F[:, 0:2, :, :], w1[:, 0:2, :, :]).then_inc(w1_in[0], 16)
            sp.dma_start(PA[:, :], attn_w).then_inc(attn_in, 16)
            sp.dma_start(W1F[:, 2:E, :, :], w1[:, 2:E, :, :]).then_inc(w1_in[1], 16)
            sp.dma_start(W2F[:, :, :], w2).then_inc(w2_in, 16)
            for h in range(HALVES):
                sp.wait_ge(summed, E * (h + 1))
                sp.dma_start(out[:, TILES * h:TILES * h + TILES, :], acc[h][:, :, :]).then_inc(out_done[h], 16)
            for h in range(HALVES):
                sp.wait_ge(out_done[h], 16)

        @block.gpsimd
        def _(pool):
            nc.gpsimd.memset(zeros[:, :], 0.0).then_inc(zeros_ready, 1)
            nc.gpsimd.memset(half[:, :], -0.5).then_inc(half_ready, 1)
            nc.gpsimd.memset(ident[:, :], 0.0).then_inc(pool_step, 1)
            pool.wait_ge(pool_step, 1)
            nc.gpsimd.affine_select(out=ident[:, :], in_=ident[:, :], compare_op=ALU.not_equal, fill=1.0,
                                    base=0, pattern=[[-1, P]], channel_multiplier=1)\
                .then_inc(ident_ready, 1)
            for h in range(HALVES):
                nc.gpsimd.memset(VH[h][:, :, C:CA], SXA * SWA)
                nc.gpsimd.memset(VL[h][:, :, C:CA], 0.0)
            nc.gpsimd.memset(ones[:, :], 1.0).then_inc(ones_ready, 1)
            for h in range(HALVES):
                pool.wait_ge(var1_ready, h + 1)
                pool.wait_ge(half_ready, 1)
                nc.gpsimd.tensor_tensor(rs1[h][:, :], base1[h][:, :], half[:, :], ALU.pow)\
                    .then_inc(rs1_ready, 1)
            for e in range(E):
                last = nc.gpsimd.memset(iota[:, e:e + 1], float(e))
            last.then_inc(iota_ready, 1)

            def scale_w1(q):
                pool.wait_ge(w1_in[min(q, 1)], 16)
                pool.wait_ge(gS_ready, 1)
                es = slice(2 * q, 2 * q + 2)
                nc.gpsimd.tensor_tensor(W1G[:, es, :, :].rearrange("p e j m -> p e (j m)"),
                                        W1F[:, es, :, :].rearrange("p e j m -> p e (j m)"),
                                        gS[:, es].unsqueeze(2).broadcast_to([P, 2, HID]),
                                        ALU.mult).then_inc(W1_scaled, 1)

            def rest_w1(q, before, done):
                pool.wait_ge(W1_hi, q + 1)
                pool.wait_ge(before, done)
                es = slice(2 * q, 2 * q + 2)
                nc.gpsimd.tensor_tensor(W1S[C:P, es, :, :], W1G[C:P, es, :, :], W1S[C:P, es, :, :],
                                        ALU.subtract).then_inc(W1_ready, 1)

            def negate_peaks(h, i):
                pool.wait_ge(peak_ready, IMG * h + i + 1)
                im = slice(PT * i, PT * i + PT)
                nc.gpsimd.tensor_scalar(nmax[h][:, im], peak[h][:, im], -1.0 / SS, None, ALU.mult)\
                    .then_inc(nmax_ready, 1)

            def add_bias(h):
                nc.gpsimd.tensor_tensor(XV[h][:, :, :], X[:, TILES * h:TILES * h + TILES, :],
                                        PA[:, A_BV:A_BV + C].unsqueeze(1).broadcast_to([P, TILES, C]),
                                        ALU.add).then_inc(xv_ready, 1)

            def second_pow(h, k, done):
                pool.wait_ge(var2_ready, h + 1)
                nc.gpsimd.tensor_tensor(rs2[h][:, k, :], base2[h][:, k, :], half[:, :], ALU.pow)\
                    .then_inc(done, 1)

            def sum_y(s):
                if sum_on_pool(s):
                    h = s // E
                    pool.wait_ge(y_used, s + 1)
                    if s % E > 0:
                        pool.wait_ge(summed, s)
                    before = T[h] if s % E == 0 else acc[h]
                    nc.gpsimd.tensor_tensor(acc[h][:, :, :], before[:, :, :], gated[:, s % GB, :, :], ALU.add)\
                        .then_inc(summed, 1)

            def rest_hidden(g):
                if sub_on_pool(g):
                    r = g % RING
                    pool.wait_ge(h32_ready, g + 1)
                    wait_hh(pool, g)
                    if g >= RING:
                        pool.wait_ge(layer2_done, g - RING + 1)
                    nc.gpsimd.tensor_tensor(HL[:, r, :], H32[:, r, :], HH[:, r, :], ALU.subtract)\
                        .then_inc(hl_pool, 1)

            scale_w1(0)
            negate_peaks(0, 0)
            scale_w1(1)
            negate_peaks(0, 1)
            scale_w1(2)
            negate_peaks(1, 0)
            negate_peaks(1, 1)
            add_bias(0)
            rest_w1(0, xv_ready, 1)
            rest_w1(1, W1_ready, 1)
            pool.wait_ge(W1_ready, 2)
            add_bias(1)
            scale_w1(3)
            second_pow(0, 0, rs2_ready)
            second_pow(0, 1, rs2b_ready)
            second_pow(1, 0, rs2_ready)
            rest_w1(2, rs2_ready, 2)
            pool.wait_ge(W1_ready, 3)
            second_pow(1, 1, rs2b_ready)
            rest_hidden(0)
            rest_hidden(1)
            rest_w1(3, hl_pool, 2)
            pool.wait_ge(W1_ready, 4)
            rest_hidden(4)
            rest_hidden(5)
            rest_hidden(6)
            rest_hidden(8)
            sum_y(0)
            rest_hidden(9)
            sum_y(1)
            rest_hidden(11)
            sum_y(2)
            for g in range(G0, G1):
                rest_hidden(g)
                for s in range(gated_before(g), gated_before(g + 1)):
                    sum_y(s)
            sum_y(9)
            sum_y(10)
            rest_hidden(28)
            sum_y(11)
            rest_hidden(31)

        @block.scalar
        def _(act):
            act.wait_ge(attn_in, 16)
            nc.scalar.mul(WA[:, :], PA[:, 0:A_BV], SWA).then_inc(WA_hi, 1)

            def round_x1(h, i):
                act.wait_ge(xn_ps, IMG * h + i + 1)
                nc.scalar.copy(X1H[h][:, PIX * i:PIX * i + PIX], ps_xn[h][i]).then_inc(X1H_ready, 1)

            def split_w1(q):
                act.wait_ge(W1_scaled, q + 1)
                nc.scalar.copy(W1S[:, 2 * q:2 * q + 2, :, :], W1G[:, 2 * q:2 * q + 2, :, :]).then_inc(W1_hi, 1)

            def round_b2():
                act.wait_ge(b2_in, 16)
                nc.scalar.mul(B2S[:, :, :], B2F[:, :, :], SW).then_inc(b2_hi, 1)

            def round_q(h):
                act.wait_ge(BA_ready, 1)
                act.wait_ge(q_ps, h + 1)
                nc.scalar.activation(QS[h][:, :], ps_q[h][0:QK, :], ACT.Identity, bias=BA[:, 0:1])\
                    .then_inc(q_hi, 1)

            def round_k(h):
                act.wait_ge(BA_ready, 1)
                act.wait_ge(k_ps, h + 1)
                nc.scalar.activation(KS[h][:, :], ps_k[h][0:QK, :], ACT.Identity, bias=BA[:, 1:2])\
                    .then_inc(k_hi, 1)

            def exps(h, i):
                act.wait_ge(nmax_ready, IMG * h + i + 1)
                for t in range(PT):
                    k = PT * i + t
                    last = nc.scalar.activation(PR[h][:, k, :], ps_S[h][i][:, t, :], ACT.Exp,
                                                bias=nmax[h][:, k:k + 1], scale=1.0 / SS)
                last.then_inc(prob_ready, 1)

            def round_probs(h, i):
                act.wait_ge(PT_ps, IMG * h + i + 1)
                nc.scalar.copy(PTH[h][:, i, :, :], ps_PT[h][i].rearrange("p (t n) -> p t n", t=PT))\
                    .then_inc(PT_hi, 1)

            def round_values(h):
                act.wait_ge(V_ps, h + 1)
                nc.scalar.copy(VH[h][:, :, 0:C], ps_V[h]).then_inc(V_hi, 1)

            def round_w2():
                act.wait_ge(w2_in, 16)
                nc.scalar.mul(W2S[:, 0, :, :], W2F[:, :, :], SW).then_inc(W2_hi, 1)

            def gelu_table():
                nc.scalar.activation(warm[:, :], half[0:1, 0:1], ACT.Gelu)

            def round_x(h, i):
                act.wait_ge(F_ps, IMG * h + i + 1)
                nc.scalar.copy(XH[h][:, PIX * i:PIX * i + PIX], ps_F[h][i]).then_inc(XH_ready, 1)

            def tanh(h):
                act.wait_ge(gap_ready, h + 1)
                nc.scalar.activation(th[h][:, :], gap[h][:, :], ACT.Tanh, scale=0.5).then_inc(th_ready, 1)

            def gelu(g):
                u, r = g % UNITS, g % RING
                if g == 0:
                    act.wait_ge(b1_ready, 2)
                act.wait_ge(z_ready, g + 1)
                if g >= RING:
                    wait_hl(act, g - RING)
                    act.wait_ge(layer2_done, g - RING + 1)
                if cast_on_act(g):
                    nc.scalar.activation(HH[:, r, :], ps_z[z_bank(g)], ACT.Gelu, bias=b1S[:, u:u + 1],
                                         scale=1.0 / (SX * SW)).then_inc(hh_act, 1)
                nc.scalar.activation(H32[:, r, :], ps_z[z_bank(g)], ACT.Gelu, bias=b1S[:, u:u + 1],
                                     scale=1.0 / (SX * SW)).then_inc(h32_ready, 1)

            round_x1(0, 0)
            round_x1(0, 1)
            round_b2()
            round_x1(1, 0)
            round_x1(1, 1)
            round_q(0)
            round_k(0)
            round_values(0)
            round_q(1)
            round_k(1)
            round_w2()
            split_w1(0)
            exps(0, 0)
            round_values(1)
            exps(0, 1)
            round_probs(0, 0)
            exps(1, 0)
            exps(1, 1)
            round_probs(0, 1)
            round_probs(1, 0)
            split_w1(1)
            round_probs(1, 1)
            split_w1(2)
            split_w1(3)
            gelu_table()
            round_x(0, 0)
            round_x(0, 1)
            gelu(0)
            round_x(1, 0)
            round_x(1, 1)
            gelu(1)
            gelu(2)
            gelu(3)
            gelu(4)
            gelu(5)
            tanh(0)
            gelu(6)
            gelu(7)
            gelu(8)
            gelu(9)
            tanh(1)
            gelu(10)
            gelu(11)
            gelu(12)
            gelu(13)
            for g in range(G0, HALVES * UNITS):
                gelu(g)

        @block.vector
        def _(dve):
            chain = [0]

            def step(ins):
                chain[0] += 1
                ins.then_inc(vec_step, 1)
                dve.wait_ge(vec_step, chain[0])

            def center(out, src, m2):
                return nc.vector.tensor_tensor(out[:, :, :], src, m2[:, :, 0:1].broadcast_to([P, TILES, C]),
                                        ALU.subtract)

            def scale_twice(out, src, rs, i):
                im = slice(PT * i, PT * i + PT)
                return nc.vector.tensor_tensor(out[:, im, :, :],
                                               src[:, im, :].unsqueeze(2).broadcast_to([P, PT, 2, C]),
                                               rs[:, im].unsqueeze(2).unsqueeze(3).broadcast_to([P, PT, 2, C]),
                                               ALU.mult)

            def first_stats(h):
                dve.wait_ge(x_in[h], 16)
                for t in range(TILES):
                    last = nc.vector.bn_stats(st[h][:, t, :], X[:, TILES * h + t, :])
                last.then_inc(st_ready, 1)

            def first_moments(h):
                dve.wait_ge(st_ready, h + 1)
                for t in range(TILES):
                    last = nc.vector.bn_aggr(mv[h][:, t, :], st[h][:, t, :])
                last.then_inc(mv_ready, 1)

            def first_variance(h):
                dve.wait_ge(mv_ready, h + 1)
                nc.vector.tensor_scalar(base1[h][:, :], mv[h][:, :, 1], EPS_C, SXA ** -2, ALU.add, ALU.mult)\
                    .then_inc(var1_ready, 1)

            def first_center(h):
                dve.wait_ge(mv_ready, h + 1)
                center(XC[h], X[:, TILES * h:TILES * h + TILES, :], mv[h]).then_inc(xc_ready, 1)

            def first_norm(h, i):
                dve.wait_ge(xc_ready, h + 1)
                dve.wait_ge(rs1_ready, h + 1)
                scale_twice(X1[h], XC[h], rs1[h], i).then_inc(x1_ready, 1)

            def small_weights():
                dve.wait_ge(WA_hi, 1)
                nc.vector.scalar_tensor_tensor(out=WA[C:P, :], in0=PA[C:P, 0:A_BV], scalar=SWA,
                                               in1=WA[C:P, :], op0=ALU.mult, op1=ALU.subtract)\
                    .then_inc(WA_ready, 1)
                nc.vector.tensor_scalar(BA[:, :], PA[0:QK, A_BQ:A_BQ + 2], SXA * SWA, None, ALU.mult)\
                    .then_inc(BA_ready, 1)

            def scale_gains():
                dve.wait_ge(ffn_in, 16)
                nc.vector.tensor_scalar(gS[:, :], PF[:, F_G:F_G + E], SW, None, ALU.mult)\
                    .then_inc(gS_ready, 1)

            def rest_x1(h, i):
                im = slice(PIX * i, PIX * i + PIX)
                dve.wait_ge(X1H_ready, IMG * h + i + 1)
                nc.vector.tensor_tensor(X1L[h][:, im], ps_xn[h][i], X1H[h][:, im], ALU.subtract)\
                    .then_inc(X1L_ready, 1)

            def rest_b2():
                dve.wait_ge(b2_hi, 1)
                nc.vector.scalar_tensor_tensor(out=B2S[DB:C, :, :], in0=B2F[DB:C, :, :], scalar=SW,
                                               in1=B2S[DB:C, :, :], op0=ALU.mult, op1=ALU.subtract)\
                    .then_inc(b2_ready, 1)

            def rest_w2(i):
                dve.wait_ge(W2_hi, 1)
                us = slice(UNITS // 2 * i, UNITS // 2 * (i + 1))
                nc.vector.scalar_tensor_tensor(out=W2S[:, 1, us, :], in0=W2F[:, us, :], scalar=SW,
                                               in1=W2S[:, 0, us, :], op0=ALU.mult, op1=ALU.subtract)\
                    .then_inc(W2_ready, 1)

            def rest_q(h):
                dve.wait_ge(BA_ready, 1)
                dve.wait_ge(q_hi, h + 1)
                nc.vector.scalar_tensor_tensor(out=QS[h][DB:2 * DB, :], in0=ps_q[h][DB:2 * DB, :],
                                               scalar=BA[DB:2 * DB, 0:1], in1=QS[h][DB:2 * DB, :],
                                               op0=ALU.add, op1=ALU.subtract).then_inc(q_ready, 1)

            def rest_k(h):
                dve.wait_ge(k_hi, h + 1)
                nc.vector.scalar_tensor_tensor(out=KS[h][2 * DB:QK, :], in0=ps_k[h][2 * DB:QK, :],
                                               scalar=BA[2 * DB:QK, 1:2], in1=KS[h][2 * DB:QK, :],
                                               op0=ALU.add, op1=ALU.subtract).then_inc(k_ready, 1)

            def take_offsets(i):
                dve.wait_ge(b1_ps, i + 1)
                us = slice(UNITS // 2 * i, UNITS // 2 * (i + 1))
                nc.vector.tensor_tensor(b1S[:, us], ps_b1[i], PF[:, F_B1 + us.start:F_B1 + us.stop],
                                        ALU.add).then_inc(b1_ready, 1)

            def peaks(h, i):
                dve.wait_ge(S_ps, IMG * h + i + 1)
                nc.vector.tensor_reduce(peak[h][:, PT * i:PT * i + PT], ps_S[h][i], AX_X, ALU.max)\
                    .then_inc(peak_ready, 1)

            def rest_values(h):
                dve.wait_ge(V_hi, h + 1)
                nc.vector.tensor_tensor(VL[h][:, :, 0:C], ps_V[h], VH[h][:, :, 0:C], ALU.subtract)\
                    .then_inc(V_ready, 1)

            def rest_probs(h, i):
                dve.wait_ge(PT_hi, IMG * h + i + 1)
                nc.vector.tensor_tensor(PTL[h][:, i, :, :], ps_PT[h][i].rearrange("p (t n) -> p t n", t=PT),
                                        PTH[h][:, i, :, :], ALU.subtract).then_inc(PT_ready, 1)

            def invert_sums(h):
                dve.wait_ge(O_ps, h + 1)
                nc.vector.reciprocal(rsum[h][:, :], ps_O[h][:, :, C]).then_inc(sums_ready, 1)

            def sum_tokens(h):
                dve.wait_ge(xv_ready, h + 1)
                dve.wait_ge(sums_ready, h + 1)
                for t in range(TILES):
                    last = nc.vector.scalar_tensor_tensor(out=T[h][:, t, :], in0=ps_O[h][:, t, 0:C],
                                                          scalar=rsum[h][:, t:t + 1], in1=XV[h][:, t, :],
                                                          op0=ALU.mult, op1=ALU.add)
                last.then_inc(t_ready, 1)

            def second_stats(h):
                dve.wait_ge(t_ready, h + 1)
                for t in range(TILES):
                    last = nc.vector.bn_stats(st2[h][:, t, :], T[h][:, t, :])
                last.then_inc(st2_ready, 1)

            def second_moments(h):
                dve.wait_ge(st2_ready, h + 1)
                for t in range(TILES):
                    last = nc.vector.bn_aggr(mv2[h][:, t, :], st2[h][:, t, :])
                last.then_inc(mv2_ready, 1)

            def second_center(h):
                dve.wait_ge(mv2_ready, h + 1)
                nc.vector.tensor_scalar(base2[h][:, 0, :], mv2[h][:, :, 1], (1.0 + EPS_T) / SX ** 2,
                                        (EPS_T / SX) ** 2, ALU.mult, ALU.add)
                nc.vector.tensor_scalar(base2[h][:, 1, :], mv2[h][:, :, 1], EPS_T, None, ALU.add)\
                    .then_inc(var2_ready, 1)
                center(TC[h], T[h][:, :, :], mv2[h]).then_inc(tc_ready, 1)

            def second_norm(h, i):
                dve.wait_ge(tc_ready, h + 1)
                dve.wait_ge(rs2_ready, h + 1)
                scale_twice(X2[h], TC[h], rs2[h][:, 0, :], i).then_inc(x2_ready, 1)

            def rest_x(h, i):
                im = slice(PIX * i, PIX * i + PIX)
                dve.wait_ge(XH_ready, IMG * h + i + 1)
                nc.vector.tensor_tensor(XL[h][:, im], ps_F[h][i], XH[h][:, im], ALU.subtract)\
                    .then_inc(XL_ready, 1)

            def route(h, stage):
                if stage == 0:
                    dve.wait_ge(rs2b_ready, h + 1)
                    step(nc.vector.reciprocal(inv2[h][:, :], rs2[h][:, 0, :]))
                    step(nc.vector.scalar_tensor_tensor(out=ratio[h][:, :], in0=rs2[h][:, 1, :],
                                                        scalar=1.0 / SWA, in1=inv2[h][:, :],
                                                        op0=ALU.mult, op1=ALU.mult))
                    dve.wait_ge(L_ps, h + 1)
                    step(nc.vector.tensor_tensor(LS[h][:, :, :], ps_L[h],
                                                 ratio[h][:, :].unsqueeze(2).broadcast_to([P, TILES, E]),
                                                 ALU.mult))
                    nc.vector.tensor_tensor(LG[h][:, :, :], LS[h][:, :, :],
                                            PF[:, F_BR:F_BR + E].unsqueeze(1).broadcast_to([P, TILES, E]),
                                            ALU.add).then_inc(logits_ready, 1)
                elif stage == 1:
                    dve.wait_ge(logits_ready, h + 1)
                    for t in range(TILES):
                        last = nc.vector.max(top[h][:, t, :], LG[h][:, t, :])
                    last.then_inc(top_ready, 1)
                elif stage == 2:
                    dve.wait_ge(top_ready, h + 1)
                    nc.vector.tensor_tensor(gap[h][:, :], top[h][:, :, 0], top[h][:, :, 1], ALU.subtract)\
                        .then_inc(gap_ready, 1)
                    for t in range(TILES):
                        last = nc.vector.max_index(topi[h][:, t, :], top[h][:, t, :], LG[h][:, t, :])
                    step(last)
                    nc.vector.tensor_copy(topf[h][:, :, :], topi[h][:, :, 0:2]).then_inc(topf_ready, 1)
                elif stage == 3:
                    dve.wait_ge(iota_ready, 1)
                    dve.wait_ge(topf_ready, h + 1)
                    for k in range(2):
                        nc.vector.tensor_tensor(hot[h][:, k, :, :],
                                                iota[:, :].unsqueeze(1).broadcast_to([P, TILES, E]),
                                                topf[h][:, :, k:k + 1].broadcast_to([P, TILES, E]),
                                                ALU.is_equal)
                    dve.wait_ge(th_ready, h + 1)
                    for k in range(2):
                        last = nc.vector.tensor_scalar(wab[h][:, k, :], th[h][:, :], (0.5 - k) * SG, 0.5 * SG,
                                                       ALU.mult, ALU.add)
                    last.then_inc(wab_ready, 1)
                elif stage == 4:
                    dve.wait_ge(wab_ready, h + 1)
                    for k in range(2):
                        last = nc.vector.tensor_tensor(part[h][:, k, :, :], hot[h][:, k, :, :],
                                                       wab[h][:, k, :].unsqueeze(2)
                                                       .broadcast_to([P, TILES, E]), ALU.mult)
                    step(last)
                    nc.vector.tensor_tensor(gate[h][:, :, :], part[h][:, 0, :, :], part[h][:, 1, :, :],
                                            ALU.add).then_inc(gate_ready, 1)

            def gate_y(s):
                h, e = s // E, s % E
                dve.wait_ge(layer2_done, J * (s + 1))
                if e == 0:
                    dve.wait_ge(gate_ready, h + 1)
                if s >= GB:
                    dve.wait_ge(summed, s - GB + 1)
                nc.vector.tensor_tensor(gated[:, s % GB, :, :], ps_y[s % YB],
                                        gate[h][:, :, e:e + 1].broadcast_to([P, TILES, C]), ALU.mult)\
                    .then_inc(y_used, 1)

            def sum_y(s):
                if not sum_on_pool(s):
                    h = s // E
                    dve.wait_ge(y_used, s + 1)
                    dve.wait_ge(summed, s)
                    nc.vector.tensor_tensor(acc[h][:, :, :], acc[h][:, :, :], gated[:, s % GB, :, :], ALU.add)\
                        .then_inc(summed, 1)

            def round_hidden(g):
                if not cast_on_act(g):
                    dve.wait_ge(h32_ready, g + 1)
                    nc.vector.tensor_copy(HH[:, g % RING, :], H32[:, g % RING, :]).then_inc(hh_dve, 1)

            def rest_hidden(g):
                if not sub_on_pool(g):
                    r = g % RING
                    dve.wait_ge(h32_ready, g + 1)
                    wait_hh(dve, g)
                    if g >= RING:
                        dve.wait_ge(layer2_done, g - RING + 1)
                    nc.vector.tensor_tensor(HL[:, r, :], H32[:, r, :], HH[:, r, :], ALU.subtract)\
                        .then_inc(hl_dve, 1)

            first_stats(0)
            first_moments(0)
            first_variance(0)
            first_stats(1)
            first_center(0)
            first_moments(1)
            first_variance(1)
            first_norm(0, 0)
            first_norm(0, 1)
            first_center(1)
            small_weights()
            first_norm(1, 0)
            first_norm(1, 1)
            rest_x1(0, 0)
            rest_x1(0, 1)
            scale_gains()
            rest_b2()
            rest_x1(1, 0)
            rest_x1(1, 1)
            rest_q(0)
            rest_k(0)
            rest_q(1)
            peaks(0, 0)
            peaks(0, 1)
            rest_k(1)
            take_offsets(0)
            rest_values(0)
            rest_values(1)
            peaks(1, 0)
            peaks(1, 1)
            rest_probs(0, 0)
            rest_w2(0)
            rest_w2(1)
            rest_probs(0, 1)
            rest_probs(1, 0)
            invert_sums(0)
            rest_probs(1, 1)
            sum_tokens(0)
            take_offsets(1)
            second_stats(0)
            invert_sums(1)
            second_moments(0)
            second_center(0)
            sum_tokens(1)
            second_norm(0, 0)
            second_stats(1)
            second_norm(0, 1)
            second_moments(1)
            second_center(1)
            rest_x(0, 0)
            rest_x(0, 1)
            second_norm(1, 0)
            second_norm(1, 1)
            round_hidden(0)
            rest_x(1, 0)
            route(0, 0)
            rest_x(1, 1)
            route(0, 1)
            route(0, 2)
            round_hidden(2)
            round_hidden(3)
            rest_hidden(2)
            rest_hidden(3)
            route(1, 0)
            route(0, 3)
            round_hidden(5)
            route(0, 4)
            route(1, 1)
            round_hidden(7)
            route(1, 2)
            rest_hidden(7)
            gate_y(0)
            route(1, 3)
            round_hidden(9)
            round_hidden(10)
            route(1, 4)
            round_hidden(11)
            gate_y(1)
            gate_y(2)
            rest_hidden(10)
            round_hidden(13)
            rest_hidden(12)
            rest_hidden(13)
            for g in range(G0, G1):
                for s in range(gated_before(g), gated_before(g + 1)):
                    gate_y(s)
                round_hidden(g)
                rest_hidden(g)
            gate_y(9)
            round_hidden(26)
            round_hidden(27)
            round_hidden(28)
            gate_y(10)
            rest_hidden(26)
            rest_hidden(27)
            gate_y(11)
            rest_hidden(29)
            gate_y(12)
            gate_y(13)
            rest_hidden(30)
            sum_y(12)
            gate_y(14)
            sum_y(13)
            sum_y(14)
            gate_y(15)
            sum_y(15)

        @block.tensor
        def _(pe):
            def keep_warm(bank, n):
                for _ in range(n):
                    nc.tensor.matmul(bank, zeros[:, 0:P], zeros[:, :], start=True, stop=True)

            pe.wait_ge(zeros_ready, 1)
            keep_warm(BK[0][0], WARM)
            pe.wait_ge(ident_ready, 1)

            def turn_x1(h, i):
                pe.wait_ge(x1_ready, IMG * h + i + 1)
                for t in range(PT):
                    last = nc.tensor.transpose(ps_xn[h][i][:, P * t:P * t + P],
                                               X1[h][:, PT * i + t, :, :].rearrange("p k c -> p (k c)"),
                                               ident[:, :])
                last.then_inc(xn_ps, 1)

            def two_parts(dst, weights, part_h, part_l):
                for n, part in enumerate((part_h, part_l)):
                    last = nc.tensor.matmul(dst, part, weights, start=(n == 0), stop=(n == 1))
                return last

            def queries_keys(h, n):
                pe.wait_ge(WA_ready, 1)
                pe.wait_ge((X1H_ready, X1L_ready)[n], IMG * (h + 1))
                part = (X1H, X1L)[n][h]
                q = nc.tensor.matmul(ps_q[h][0:QK, :], WA[:, A_WQ:A_WQ + QK], part[:, :],
                                     start=(n == 0), stop=(n == 1))
                if n == 1:
                    q.then_inc(q_ps, 1)
                k = nc.tensor.matmul(ps_k[h][0:QK, :], WA[:, A_WK:A_WK + QK], part[:, :],
                                     start=(n == 0), stop=(n == 1))
                if n == 1:
                    k.then_inc(k_ps, 1)

            def values(h):
                pe.wait_ge(X1L_ready, IMG * (h + 1))
                for t in range(TILES):
                    ts = slice(P * t, P * t + P)
                    last = two_parts(ps_V[h][:, t, :], WA[:, A_WV:A_WV + C], X1H[h][:, ts], X1L[h][:, ts])
                last.then_inc(V_ps, 1)

            def offsets(first, end):
                pe.wait_ge(ffn_in, 16)
                for u in range(first, end):
                    i, c = divmod(u, UNITS // 2)
                    pe.wait_ge(w1_in[0 if u < 2 * J else 1], 16)
                    last = nc.tensor.matmul(ps_b1[i][:, c:c + 1], W1F[:, u // J, u % J, :],
                                            PF[:, F_B + u // J:F_B + u // J + 1], start=True, stop=True)
                    if c == UNITS // 2 - 1:
                        last.then_inc(b1_ps, 1)

            def scores(h, i):
                if h == 1 and i == 0:
                    pe.wait_ge(b1_ready, 1)
                pe.wait_ge(q_ready, h + 1)
                pe.wait_ge(k_ready, h + 1)
                for t in range(PT):
                    k = PT * i + t
                    last = nc.tensor.matmul(ps_S[h][i][:, t, :], QS[h][:, P * k:P * k + P],
                                            KS[h][:, PIX * i:PIX * i + PIX], start=True, stop=True)
                last.then_inc(S_ps, 1)

            def turn_probs(h, i):
                pe.wait_ge(prob_ready, IMG * h + i + 1)
                if i == 1:
                    pe.wait_ge(V_ready, h + 1)
                for t in range(PT):
                    for m in range(PT):
                        c = PIX * m + P * t
                        last = nc.tensor.transpose(ps_PT[h][i][:, c:c + P], PR[h][:, PT * i + t, P * m:P * m + P],
                                                   ident[:, :])
                last.then_inc(PT_ps, 1)

            def attend(h, i):
                pe.wait_ge(ones_ready, 1)
                pe.wait_ge(V_ready, h + 1)
                pe.wait_ge(PT_ready, IMG * h + i + 1)
                for t in range(PT):
                    k = PT * i + t
                    for m in range(PT):
                        ph = PTH[h][:, i, m, P * t:P * t + P]
                        pl = PTL[h][:, i, m, P * t:P * t + P]
                        vh, vl = VH[h][:, PT * i + m, :], VL[h][:, PT * i + m, :]
                        nc.tensor.matmul(ps_O[h][:, k, 0:CA], ph, vh, start=(m == 0), stop=False)
                        nc.tensor.matmul(ps_O[h][:, k, 0:CA], ph, vl, start=False, stop=False)
                        last = nc.tensor.matmul(ps_O[h][:, k, 0:CA], pl, vh, start=False, stop=(m == PT - 1))
                if i == IMG - 1:
                    last.then_inc(O_ps, 1)

            def turn_x(h, i):
                pe.wait_ge(b1_ready, 2)
                pe.wait_ge(x2_ready, IMG * h + i + 1)
                for t in range(PT):
                    last = nc.tensor.transpose(ps_F[h][i][:, P * t:P * t + P],
                                               X2[h][:, PT * i + t, :, :].rearrange("p k c -> p (k c)"),
                                               ident[:, :])
                last.then_inc(F_ps, 1)

            def logits(h):
                pe.wait_ge(XL_ready, IMG * (h + 1))
                for t in range(TILES):
                    ts = slice(P * t, P * t + P)
                    last = two_parts(ps_L[h][:, t, :], WA[:, A_WR:A_WR + E], XH[h][:, ts], XL[h][:, ts])
                last.then_inc(L_ps, 1)

            def layer1(g):
                h, e, j = g // UNITS, (g % UNITS) // J, g % J
                pe.wait_ge(W1_ready, e // 2 + 1)
                if g in (0, GZ + 2):
                    pe.wait_ge(XL_ready, IMG if g == 0 else 2 * IMG)
                before = [n for n in range(g) if z_bank(n) == z_bank(g)]
                if before:
                    pe.wait_ge(h32_ready, before[-1] + 1)
                nc.tensor.matmul(ps_z[z_bank(g)], W1S[:, e, j, :], XH[h][:, :], start=True, stop=False)
                nc.tensor.matmul(ps_z[z_bank(g)], W1S[:, e, j, :], XL[h][:, :], start=False, stop=True)\
                    .then_inc(z_ready, 1)

            def layer2(g):
                u, j, s = g % UNITS, g % J, g // J
                if j == 0 and s >= YB:
                    pe.wait_ge(y_used, s - YB + 1)
                if j == 0 and s < YB and s % 2 == 1:
                    pe.wait_ge(logits_ready, s // 2 + 1)
                if g in (0, UNITS // 2):
                    pe.wait_ge(W2_ready, 1 + g // (UNITS // 2))
                    pe.wait_ge(b2_ready, 1)
                if j == 0:
                    nc.tensor.matmul(ps_y[s % YB], ones[:, :],
                                     B2S[:, u // J, :].unsqueeze(1).broadcast_to([C, TILES, C]),
                                     start=True, stop=False, skip_group_check=True)
                wait_hh(pe, g)
                wait_hl(pe, g)
                for t in range(TILES):
                    hh = HH[:, g % RING, P * t:P * t + P]
                    hl = HL[:, g % RING, P * t:P * t + P]
                    nc.tensor.matmul(ps_y[s % YB][:, t, :], hh, W2S[:, 0, u, :],
                                     start=False, stop=False, skip_group_check=True)
                    nc.tensor.matmul(ps_y[s % YB][:, t, :], hh, W2S[:, 1, u, :],
                                     start=False, stop=False, skip_group_check=True)
                    last = nc.tensor.matmul(ps_y[s % YB][:, t, :], hl, W2S[:, 0, u, :],
                                            start=False, stop=(j == J - 1), skip_group_check=True)
                last.then_inc(layer2_done, 1)

            turn_x1(0, 0)
            turn_x1(0, 1)
            turn_x1(1, 0)
            turn_x1(1, 1)
            queries_keys(0, 0)
            queries_keys(0, 1)
            values(0)
            queries_keys(1, 0)
            queries_keys(1, 1)
            values(1)
            offsets(0, 4)
            scores(0, 0)
            scores(0, 1)
            offsets(4, 7)
            keep_warm(ps_PT[0][0], 3)
            offsets(7, 8)
            keep_warm(ps_PT[0][0], 3)
            scores(1, 0)
            scores(1, 1)
            turn_probs(0, 0)
            turn_probs(0, 1)
            turn_probs(1, 0)
            offsets(8, 10)
            turn_probs(1, 1)
            offsets(10, 11)
            attend(0, 0)
            attend(0, 1)
            offsets(11, 16)
            attend(1, 0)
            attend(1, 1)
            keep_warm(ps_PT[0][0], 3)
            keep_warm(ps_PT[0][0], 3)
            turn_x(0, 0)
            keep_warm(ps_PT[0][0], 3)
            turn_x(0, 1)
            layer1(0)
            turn_x(1, 0)
            turn_x(1, 1)
            layer1(1)
            logits(0)
            layer1(2)
            layer1(3)
            layer1(4)
            layer1(5)
            layer1(6)
            layer2(0)
            logits(1)
            layer1(7)
            layer2(1)
            layer2(2)
            layer1(8)
            layer1(9)
            layer1(10)
            layer2(3)
            layer2(4)
            layer1(11)
            layer1(12)
            layer1(13)
            layer2(5)
            layer2(6)
            layer2(7)
            for g in range(G0, G1):
                layer1(g)
                layer2(g - LAG)
            layer1(26)
            layer1(27)
            layer2(20)
            layer1(28)
            layer2(21)
            layer1(29)
            layer1(30)
            layer2(22)
            layer1(31)
            layer2(23)
            layer2(24)
            layer2(25)
            layer2(26)
            layer2(27)
            layer2(28)
            layer2(29)
            layer2(30)
            layer2(31)


_OUTS = [((P, IMAGES * PT, C), 'float32')]


def laid_out(x, L0_conv_wq, L0_conv_bq, L0_conv_wk, L0_conv_bk, L0_conv_wv, L0_conv_bv, L0_ffn_Wr,
             L0_ffn_br, L0_ffn_ln_g, L0_ffn_ln_b, L0_ffn_W1, L0_ffn_b1, L0_ffn_W2, L0_ffn_b2):
    import numpy as np

    tokens = x.reshape(IMAGES, C, PT, P).transpose(3, 0, 2, 1).reshape(P, IMAGES * PT, C)
    a = np.zeros((P, A_END), np.float32)
    f = np.zeros((P, F_END), np.float32)
    for top in (0, C):
        rows = slice(top, top + C)
        for b in range(3):
            a[rows, A_WQ + DB * b:A_WQ + DB * b + D] = L0_conv_wq.T
            a[rows, A_WK + DB * b:A_WK + DB * b + D] = L0_conv_wk.T
        a[rows, A_WV:A_WV + C] = L0_conv_wv.T
        a[rows, A_WR:A_WR + E] = L0_ffn_Wr
        f[rows, F_G:F_G + E] = L0_ffn_ln_g.T
    f[0:C, F_B:F_B + E] = L0_ffn_ln_b.T
    for b in range(3):
        a[DB * b:DB * b + D, A_BQ] = L0_conv_bq
        a[DB * b:DB * b + D, A_BK] = L0_conv_bk
    a[:, A_BV:A_BV + C] = L0_conv_bv
    f[:, F_B1:F_B1 + UNITS] = L0_ffn_b1.reshape(UNITS, P).T
    f[:, F_BR:F_BR + E] = L0_ffn_br
    b2 = np.zeros((C, E, C), np.float32)
    b2[0] = b2[DB] = L0_ffn_b2
    w1 = L0_ffn_W1.transpose(1, 0, 2).reshape(1, C, E, J, P)
    w1 = np.concatenate([w1, w1]).reshape(P, E, J, P)
    w2 = L0_ffn_W2.reshape(UNITS, P, C).transpose(1, 0, 2)
    return {"x": tokens, "attn_w": a, "ffn_w": f, "w1": w1, "w2": w2, "b2": b2}


def kernel(**inputs):
    import numpy as _np
    import concourse.bacc as _bacc
    from concourse import mybir as _mybir
    from concourse.bass_utils import run_bass_kernel_spmd as _run

    nc = _bacc.Bacc("TRN2", target_bir_lowering=False, num_devices=1)
    arrays, args = {}, []
    for name, a in laid_out(**{k: _np.asarray(v) for k, v in inputs.items()}).items():
        a = _np.ascontiguousarray(a)
        arrays[f"in_{name}_dram"] = a
        args.append(nc.dram_tensor(f"in_{name}_dram", a.shape, _mybir.dt.from_np(a.dtype), kind="ExternalInput").ap())
    for i, (shape, dtype) in enumerate(_OUTS):
        dt = _mybir.dt.from_np(_np.dtype(dtype))
        args.append(nc.dram_tensor(f"out_{i}_dram", shape, dt, kind="ExternalOutput").ap())
    build_block(nc, *args)
    r = _run(nc, [arrays], core_ids=[0])
    got = tuple(r.results[0][f"out_{i}_dram"] for i in range(len(_OUTS)))
    return got[0].reshape(P, IMAGES, PT, C).transpose(1, 3, 2, 0).reshape(IMAGES, C, 16, 16)
```
